# Optimizing a Trainium2 kernel written in Bass

```python
import numpy as np
import jax
import jax.numpy as jnp

def _softmax(x, axis=-1):
    return jax.nn.softmax(x, axis=axis)

def _gelu(x):
    return jax.nn.gelu(x, approximate=True)

def _silu(x):
    return jax.nn.silu(x)

def _sigmoid(x):
    return jax.nn.sigmoid(x)

def _layernorm(x, axis=-1, eps=1e-05):
    m = jnp.mean(x, axis=axis, keepdims=True)
    v = jnp.var(x, axis=axis, keepdims=True)
    return (x - m) / jnp.sqrt(v + eps)

def _scatter_add(tgt, idx, src, axis=0):
    return tgt.at[idx].add(src)

def _segment_sum(src, seg, n):
    return jax.ops.segment_sum(src, seg, n)
kernel_name = 'mk_audio_tower_d2_tok_audfeat512_r4_273de5'

def setup_inputs(seed: int=0):
    np.random.seed(seed)
    _w = jnp.asarray

    def _rec_inputs():
        import jax
        import jax.numpy as jnp
        _rk = jax.random.key(seed)
        x = -0.000605797 + 1.00053 * jax.random.normal(jax.random.fold_in(_rk, 1), (32, 250, 64), jnp.float32)
        return x
    x = _rec_inputs()

    def _L0_tok_setup():
        import jax, jax.numpy as jnp
        import numpy as np
        PATCH_SIZES = [4, 8, 16]
        B, S, D, H = (32, 250, 64, 128)
        key = jax.random.key(seed)
        ks = jax.random.split(key, 8)
        inp = {'x': jax.random.normal(ks[0], (B, S, D), dtype=jnp.float32)}
        for i, p in enumerate(PATCH_SIZES):
            fan_in = p * D
            inp[f'W{i}'] = jax.random.normal(ks[1 + 2 * i], (H, fan_in), dtype=jnp.float32) / np.sqrt(fan_in).astype(np.float32)
            inp[f'b{i}'] = jax.random.normal(ks[2 + 2 * i], (H,), dtype=jnp.float32) * 0.01
        inp['pos'] = jax.random.normal(ks[7], (1, 250, H), dtype=jnp.float32)
        return inp
    _L0_tok_all = _L0_tok_setup()
    _L0_tok_in = {k: v for k, v in _L0_tok_all.items() if k in ('W0', 'b0', 'W1', 'b1', 'W2', 'b2', 'pos')}
    del _L0_tok_all

    def _L0_attn_setup():
        import jax, jax.numpy as jnp
        import numpy as np
        DT = 0.01
        DAMP_MIN = 0.0005
        key = jax.random.key(seed)
        ks = jax.random.split(key, 6)
        B_batch, L, Din, N = (4, 1024, 128, 64)
        u = jax.random.normal(ks[0], (B_batch, L, Din), dtype=jnp.float32)
        A_real = jax.random.normal(ks[1], (N,), dtype=jnp.float32) * 0.1 - DAMP_MIN
        A_imag = jax.random.normal(ks[2], (N,), dtype=jnp.float32)
        B_mat = jax.random.normal(ks[3], (N, Din), dtype=jnp.float32) * 0.02
        C_mat = jax.random.normal(ks[4], (Din, N), dtype=jnp.float32) * 0.02
        D_vec = jax.random.normal(ks[5], (Din,), dtype=jnp.float32)
        return {'u': u, 'A_real': A_real, 'A_imag': A_imag, 'B_mat': B_mat, 'C_mat': C_mat, 'D_vec': D_vec}
    _L0_attn_all = _L0_attn_setup()
    _L0_attn_in = {k: v for k, v in _L0_attn_all.items() if k in ('A_real', 'A_imag', 'B_mat', 'C_mat', 'D_vec')}
    del _L0_attn_all

    def _L0_ffn_setup():
        import jax, jax.numpy as jnp
        import numpy as np
        B, S, D, E, O = (256, 64, 128, 16, 128)
        key = jax.random.key(seed)
        k_x, k_wg, k_bg, k_we, k_be = jax.random.split(key, 5)
        scale_g = 1.0 / np.sqrt(D)
        scale_e = 1.0 / np.sqrt(D)
        return {'x': jax.random.normal(k_x, (B, S, D), dtype=jnp.float32), 'Wg': jax.random.uniform(k_wg, (D, E), jnp.float32, -scale_g, scale_g), 'bg': jax.random.uniform(k_bg, (E,), jnp.float32, -scale_g, scale_g), 'We': jax.random.uniform(k_we, (E, D, O), jnp.float32, -scale_e, scale_e), 'be': jax.random.uniform(k_be, (E, O), jnp.float32, -scale_e, scale_e)}
    _L0_ffn_all = _L0_ffn_setup()
    _L0_ffn_in = {k: v for k, v in _L0_ffn_all.items() if k in ('Wg', 'bg', 'We', 'be')}
    del _L0_ffn_all

    def _L1_attn_setup():
        import jax, jax.numpy as jnp
        import numpy as np
        B, S, D = (8, 1024, 128)
        EPS = 1e-06

        def _forward(x_seq, Wq, bq, Wk, bk, Wv, bv, Wa, ba):
            q = jax.nn.relu(jnp.einsum('bsd,ed->bse', x_seq, Wq) + bq)
            k = jax.nn.relu(jnp.einsum('bsd,ed->bse', x_seq, Wk) + bk)
            v = jnp.einsum('bsd,ed->bse', x_seq, Wv) + bv
            a = jax.nn.sigmoid(jnp.einsum('bsd,ed->bse', x_seq, Wa) + ba)
            qs, ks_, vs, as_ = (jnp.swapaxes(t, 0, 1) for t in (q, k, v, a))

            def step(carry, inp):
                s, z = carry
                q_t, k_t, v_t, a_t = inp
                s = a_t[:, :, None] * s + k_t[:, :, None] * v_t[:, None, :]
                z = a_t * z + k_t
                num = jnp.einsum('bi,bij->bj', q_t, s)
                den = jnp.sum(q_t * z, axis=-1, keepdims=True) + EPS
                return ((s, z), num / den)
            s0 = jnp.zeros((x_seq.shape[0], x_seq.shape[2], x_seq.shape[2]), x_seq.dtype)
            z0 = jnp.zeros((x_seq.shape[0], x_seq.shape[2]), x_seq.dtype)
            _, ys = jax.lax.scan(step, (s0, z0), (qs, ks_, vs, as_))
            return jnp.swapaxes(ys, 0, 1)
        key = jax.random.key(seed)
        ks = jax.random.split(key, 9)
        scale = 1.0 / np.sqrt(D)
        inp = {'x_seq': jax.random.normal(ks[0], (B, S, D), dtype=jnp.float32), 'Wq': jax.random.uniform(ks[1], (D, D), jnp.float32, -scale, scale), 'bq': jax.random.uniform(ks[2], (D,), jnp.float32, -scale, scale), 'Wk': jax.random.uniform(ks[3], (D, D), jnp.float32, -scale, scale), 'bk': jax.random.uniform(ks[4], (D,), jnp.float32, -scale, scale), 'Wv': jax.random.uniform(ks[5], (D, D), jnp.float32, -scale, scale), 'bv': jax.random.uniform(ks[6], (D,), jnp.float32, -scale, scale), 'Wa': jax.random.uniform(ks[7], (D, D), jnp.float32, -scale, scale), 'ba': jax.random.uniform(ks[8], (D,), jnp.float32, -scale, scale)}
        return inp
    _L1_attn_all = _L1_attn_setup()
    _L1_attn_in = {k: v for k, v in _L1_attn_all.items() if k in ('Wq', 'bq', 'Wk', 'bk', 'Wv', 'bv', 'Wa', 'ba')}
    del _L1_attn_all

    def _L1_ffn_setup():
        import jax, jax.numpy as jnp
        import numpy as np
        CAPACITY_FACTOR = 1.2
        key = jax.random.key(seed)
        k1, k2, k3 = jax.random.split(key, 3)
        B, S, D, E = (8, 1024, 128, 16)
        x = jax.random.normal(k1, (B, S, D), dtype=jnp.float32)
        switch_w = jax.random.normal(k2, (E, D), dtype=jnp.float32) * 0.02
        switch_b = jnp.zeros((E,), dtype=jnp.float32)
        expert_w = jax.random.normal(k3, (E, D, D), dtype=jnp.float32) * 0.02
        expert_b = jnp.zeros((E, D), dtype=jnp.float32)
        return {'x': x, 'switch_w': switch_w, 'switch_b': switch_b, 'expert_w': expert_w, 'expert_b': expert_b}
    _L1_ffn_all = _L1_ffn_setup()
    _L1_ffn_in = {k: v for k, v in _L1_ffn_all.items() if k in ('switch_w', 'switch_b', 'expert_w', 'expert_b')}
    del _L1_ffn_all
    return {'x': x, 'L0_tok_W0': _L0_tok_in['W0'], 'L0_tok_b0': _L0_tok_in['b0'], 'L0_tok_W1': _L0_tok_in['W1'], 'L0_tok_b1': _L0_tok_in['b1'], 'L0_tok_W2': _L0_tok_in['W2'], 'L0_tok_b2': _L0_tok_in['b2'], 'L0_tok_pos': _L0_tok_in['pos'], 'L0_attn_A_real': _L0_attn_in['A_real'], 'L0_attn_A_imag': _L0_attn_in['A_imag'], 'L0_attn_B_mat': _L0_attn_in['B_mat'], 'L0_attn_C_mat': _L0_attn_in['C_mat'], 'L0_attn_D_vec': _L0_attn_in['D_vec'], 'L0_ffn_Wg': _L0_ffn_in['Wg'], 'L0_ffn_bg': _L0_ffn_in['bg'], 'L0_ffn_We': _L0_ffn_in['We'], 'L0_ffn_be': _L0_ffn_in['be'], 'L1_attn_Wq': _L1_attn_in['Wq'], 'L1_attn_bq': _L1_attn_in['bq'], 'L1_attn_Wk': _L1_attn_in['Wk'], 'L1_attn_bk': _L1_attn_in['bk'], 'L1_attn_Wv': _L1_attn_in['Wv'], 'L1_attn_bv': _L1_attn_in['bv'], 'L1_attn_Wa': _L1_attn_in['Wa'], 'L1_attn_ba': _L1_attn_in['ba'], 'L1_ffn_switch_w': _L1_ffn_in['switch_w'], 'L1_ffn_switch_b': _L1_ffn_in['switch_b'], 'L1_ffn_expert_w': _L1_ffn_in['expert_w'], 'L1_ffn_expert_b': _L1_ffn_in['expert_b']}

def reference(x, L0_tok_W0, L0_tok_b0, L0_tok_W1, L0_tok_b1, L0_tok_W2, L0_tok_b2, L0_tok_pos, L0_attn_A_real, L0_attn_A_imag, L0_attn_B_mat, L0_attn_C_mat, L0_attn_D_vec, L0_ffn_Wg, L0_ffn_bg, L0_ffn_We, L0_ffn_be, L1_attn_Wq, L1_attn_bq, L1_attn_Wk, L1_attn_bk, L1_attn_Wv, L1_attn_bv, L1_attn_Wa, L1_attn_ba, L1_ffn_switch_w, L1_ffn_switch_b, L1_ffn_expert_w, L1_ffn_expert_b):
    import jax
    import jax.numpy as jnp

    def _L0_tok_ref(x, W0, b0, W1, b1, W2, b2, pos):
        import jax, jax.numpy as jnp
        import numpy as np
        PATCH_SIZES = [4, 8, 16]
        B, S, D, H = (32, 250, 64, 128)
        Ws = [W0, W1, W2]
        bs = [b0, b1, b2]
        batch, seq_len, d = x.shape
        min_len = seq_len - max(PATCH_SIZES) + 1
        embs = []
        for p, W, b in zip(PATCH_SIZES, Ws, bs):
            idx = jnp.arange(min_len)[:, None] + jnp.arange(p)[None, :]
            win = x[:, idx, :]
            Wk = W.reshape(-1, p, d)
            embs.append(jnp.einsum('blpd,hpd->blh', win, Wk) + b)
        out = jnp.stack(embs, axis=1).mean(axis=1)
        return out + pos[:, :min_len, :]

    def _L0_attn_ref(u, A_real, A_imag, B_mat, C_mat, D_vec):
        import jax, jax.numpy as jnp
        import numpy as np
        DT = 0.01
        DAMP_MIN = 0.0005
        L = u.shape[1]
        a_real = -jnp.abs(A_real) - DAMP_MIN
        A = jax.lax.complex(a_real, A_imag)
        denom = 1.0 - DT * 0.5 * A
        A_bar = (1.0 + DT * 0.5 * A) / denom
        B_bar = DT * B_mat.astype(jnp.complex64) / denom[:, None]
        k = jnp.arange(L, dtype=jnp.float32)
        A_pow = A_bar[:, None] ** k[None, :]
        v = jnp.einsum('bld,nd->bln', u.astype(jnp.complex64), B_bar)
        n_fft = 2 * L
        v_f = jnp.fft.fft(v, n=n_fft, axis=1)
        k_f = jnp.fft.fft(A_pow.T, n=n_fft, axis=0)
        y = jnp.fft.ifft(v_f * k_f[None, :, :], axis=1)[:, :L, :]
        y_out = jnp.einsum('bln,dn->bld', y, C_mat.astype(jnp.complex64)).real
        return y_out + u * D_vec

    def _L0_ffn_ref(x, Wg, bg, We, be):
        import jax, jax.numpy as jnp
        import numpy as np
        B, S, D, E, O = (256, 64, 128, 16, 128)
        scores = jax.nn.softmax(jnp.mean(x, axis=1) @ Wg + bg, axis=-1)
        idx = jnp.argmax(scores, axis=-1)
        gate = jnp.take_along_axis(scores, idx[:, None], axis=-1)
        W_sel = We[idx]
        b_sel = be[idx]
        y = jnp.einsum('bsd,bdo->bso', x, W_sel) + b_sel[:, None, :]
        return gate[:, :, None] * y

    def _L1_attn_ref(x_seq, Wq, bq, Wk, bk, Wv, bv, Wa, ba):
        import jax, jax.numpy as jnp
        import numpy as np
        B, S, D = (8, 1024, 128)
        EPS = 1e-06

        def _forward(x_seq, Wq, bq, Wk, bk, Wv, bv, Wa, ba):
            q = jax.nn.relu(jnp.einsum('bsd,ed->bse', x_seq, Wq) + bq)
            k = jax.nn.relu(jnp.einsum('bsd,ed->bse', x_seq, Wk) + bk)
            v = jnp.einsum('bsd,ed->bse', x_seq, Wv) + bv
            a = jax.nn.sigmoid(jnp.einsum('bsd,ed->bse', x_seq, Wa) + ba)
            qs, ks_, vs, as_ = (jnp.swapaxes(t, 0, 1) for t in (q, k, v, a))

            def step(carry, inp):
                s, z = carry
                q_t, k_t, v_t, a_t = inp
                s = a_t[:, :, None] * s + k_t[:, :, None] * v_t[:, None, :]
                z = a_t * z + k_t
                num = jnp.einsum('bi,bij->bj', q_t, s)
                den = jnp.sum(q_t * z, axis=-1, keepdims=True) + EPS
                return ((s, z), num / den)
            s0 = jnp.zeros((x_seq.shape[0], x_seq.shape[2], x_seq.shape[2]), x_seq.dtype)
            z0 = jnp.zeros((x_seq.shape[0], x_seq.shape[2]), x_seq.dtype)
            _, ys = jax.lax.scan(step, (s0, z0), (qs, ks_, vs, as_))
            return jnp.swapaxes(ys, 0, 1)
        return _forward(x_seq, Wq, bq, Wk, bk, Wv, bv, Wa, ba)

    def _L1_ffn_ref(x, switch_w, switch_b, expert_w, expert_b):
        import jax, jax.numpy as jnp
        import numpy as np
        CAPACITY_FACTOR = 1.2
        B, S, D = x.shape
        E = switch_w.shape[0]
        N = B * S
        xf = x.reshape(N, D)
        logits = xf @ switch_w.T + switch_b
        probs = jax.nn.softmax(logits, axis=-1)
        route_probs = jnp.max(probs, axis=-1)
        routes = jnp.argmax(probs, axis=-1)
        oh = jax.nn.one_hot(routes, E, dtype=jnp.int32)
        pos = jnp.take_along_axis(jnp.cumsum(oh, axis=0), routes[:, None], axis=1)[:, 0] - 1
        capacity = int(CAPACITY_FACTOR * N / E)
        keep = pos < capacity
        buf = jnp.zeros((E, capacity, D), dtype=xf.dtype).at[routes, pos].set(xf)
        y = jnp.einsum('ecd,efd->ecf', buf, expert_w) + expert_b[:, None, :]
        gathered = y[routes, jnp.minimum(pos, capacity - 1)]
        out = jnp.where(keep[:, None], gathered, xf) * route_probs[:, None]
        return out.reshape(B, S, D)
    h = _L0_tok_ref(x, L0_tok_W0, L0_tok_b0, L0_tok_W1, L0_tok_b1, L0_tok_W2, L0_tok_b2, L0_tok_pos)
    h = h + _L0_attn_ref(_layernorm(h, axis=-1), L0_attn_A_real, L0_attn_A_imag, L0_attn_B_mat, L0_attn_C_mat, L0_attn_D_vec)
    h = h + _L0_ffn_ref(_layernorm(h, axis=-1), L0_ffn_Wg, L0_ffn_bg, L0_ffn_We, L0_ffn_be)
    h = h + _L1_attn_ref(_layernorm(h, axis=-1), L1_attn_Wq, L1_attn_bq, L1_attn_Wk, L1_attn_bk, L1_attn_Wv, L1_attn_bv, L1_attn_Wa, L1_attn_ba)
    h = h + _L1_ffn_ref(_layernorm(h, axis=-1), L1_ffn_switch_w, L1_ffn_switch_b, L1_ffn_expert_w, L1_ffn_expert_b)
    return h

_drawn_inputs = setup_inputs


def setup_inputs(seed=0):
    import zlib

    import numpy as np

    out = dict(_drawn_inputs(seed))
    spreads = {'L1_ffn_switch_b': (0.0, 0.304), 'L1_ffn_expert_b': (0.0, 0.8)}
    factors = {'L0_tok_b0': 8.0,
     'L0_tok_b1': 5.995,
     'L0_tok_b2': 7.855,
     'L0_attn_A_real': 8.0,
     'L0_attn_A_imag': 8.0,
     'L0_attn_B_mat': 8.0,
     'L0_attn_C_mat': 8.0,
     'L0_ffn_be': 23.005,
     'L1_attn_bq': 8.0,
     'L1_attn_bk': 8.0,
     'L1_attn_Wa': 6.32,
     'L1_attn_ba': 47.579,
     'L1_ffn_expert_w': 4.84}
    for name, (base, spread) in spreads.items():
        noise = np.random.default_rng([zlib.crc32(name.encode()), seed]).standard_normal(out[name].shape)
        drawn = base * np.exp(spread * noise) if base else spread * noise
        out[name] = jnp.asarray(drawn.astype(out[name].dtype))
    for name, factor in factors.items():
        out[name] = (out[name] * factor).astype(out[name].dtype)
    return out
```

```python
from contextlib import ExitStack

import concourse.bass as bass
from concourse import mybir

ALU = mybir.AluOpType
ACT = mybir.ActivationFunctionType
AX_X = mybir.AxisListType.X
F32 = mybir.dt.float32
BF16 = mybir.dt.bfloat16
I32 = mybir.dt.int32

P = 128
B = 32
S_IN = 250
D_IN = 64
PATCH = 16
L = S_IN - PATCH + 1
BU = 2
W = BU * L
U = B // BU
NTOK = B * L
TAPS = PATCH // 2
XT = S_IN - 1
N_STATE = 64
E = 16
LN_EPS = 1e-5
ATTN_EPS = 1e-6
TILE = 128
TPB = 2
LP = TPB * TILE
NT = BU * TPB
RT = 94
RM = W // RT
CAP = int(1.2 * NTOK / E)
ET = 113
EM = -(-CAP // ET)
REGION = ET * EM
ROW = 2 * P + 2
NOWHERE = 1.0e6
DT = 0.01
DAMP_MIN = 0.0005
LN_EXP = "natural_log_exp_and_others"
WB_IN = 16 * 9
PADS = 2 * 4 + 2
R_STEPS = 15

LEVELS = [1, 2, 4, 8, 16]
CONSTS = [("ident", P), ("center", P), ("mean", P), ("ones", P), ("upper", P), ("diag32", 32)] + \
    [(f"level{s}", 32) for s in LEVELS] + [("first_wins", E), ("slot_base", E), ("expert_id", E), ("token", RM)]
C_OFF = {}
C_W = 0
for _n, _w in CONSTS:
    C_OFF[_n] = (C_W, C_W + _w)
    C_W += _w


def bass_audio_tower_kernel(nc, ins, slots, out):
    ctx = ExitStack()
    with ctx:
        def sb(name, shape, dt=F32):
            return ctx.enter_context(nc.sbuf_tensor(name, shape, dt))

        def pb(name, n=1):
            return ctx.enter_context(nc.psum_tensor(name, [P, n, 512], F32))

        def sem(name):
            return ctx.enter_context(nc.semaphore(name))

        cst = sb("cst", [P, C_W])

        def const(name):
            a, b = C_OFF[name]
            return cst[:, a:b]

        h = sb("h", [P, NTOK])
        u2 = sb("u2", [P, NTOK])
        xin = [sb(f"xin{i}", [P, BU, XT]) for i in range(2)]
        wconv = sb("wconv", [P, TAPS, P])
        wconv1 = sb("wconv1", [P, TAPS // 2, P])
        wconv0 = sb("wconv0", [P, TAPS // 4, P])
        posb = sb("posb", [P, L])
        cols = sb("cols", [P, 16])
        ssm_in = sb("ssm_in", [P, P])
        ssm_out = sb("ssm_out", [P, P])
        tab = sb("tab", [P, 24])
        cosn = sb("cosn", [P, 256])
        sinn = sb("sinn", [P, 256])
        tmpn = sb("tmpn", [P, 256])
        tin = sb("tin", [P, L])
        tout = sb("tout", [P, L])
        decay = sb("decay", [P, BU, L])
        sq = sb("sq", [P, W])
        std = sb("std", [P, W])
        rstd = sb("rstd", [P, W])
        sq2 = sb("sq2", [P, W])
        std2 = sb("std2", [P, W])
        rstd2 = sb("rstd2", [P, W])
        u1 = sb("u1", [P, W])
        vin = sb("vin", [P, W])
        state = sb("state", [P, W])
        msum = sb("msum", [P, B])
        eps = sb("eps", [P, 1])

        wg = sb("wg", [P, E])
        gate_b = sb("gate_b", [B, E])
        be0 = sb("be0", [E, P])
        gs = sb("gs", [B, 8 * E])
        gT = sb("gT", [E, B])
        pick_f = sb("pick_f", [B, 1])
        pick = sb("pick", [1, B], I32)
        gate = sb("gate", [P, B])
        gbias = sb("gbias", [P, B])
        wsel = [sb(f"wsel{i}", [P, BU, P]) for i in range(2)]
        ffn = sb("ffn", [P, W])
        wqkav = sb("wqkav", [P, 4, P])
        bv = sb("bv", [P, P])
        u3 = sb("u3", [P, BU, LP])
        q = [sb(f"q{i}", [P, BU, LP]) for i in range(2)]
        k = [sb(f"k{i}", [P, BU, LP]) for i in range(2)]
        a = [sb(f"a{i}", [P, BU, LP]) for i in range(2)]
        v = [sb(f"v{i}", [P, NT, P + 1]) for i in range(2)]
        qs = sb("qs", [P, BU * LP])
        prod = {n: sb(f"prod{n}", [P, BU * LP // n]) for n in (2, 4, 8, 16, 32, 64)}
        near = sb("near", [P, NT, 32])
        attn = sb("attn", [P, BU, 3, P])
        den = sb("den", [P, BU, TPB])
        rden = sb("rden", [P, BU, TPB])
        mixed = sb("mixed", [P, NT, P])
        h3 = [sb(f"h3_{i}", [P, W]) for i in range(2)]
        u4 = sb("u4", [P, W])
        wswitch = sb("wswitch", [P, E])
        bswitch = sb("bswitch", [RT, E])
        upper_bf = sb("upper_bf", [RT, RT], BF16)
        ones_bf = sb("ones_bf", [RT, RT], BF16)
        r1 = {n: sb(f"r_{n}", [RT, RM, E]) for n in "logit shifted exps first cand rank ranked based".split()}
        onehot = sb("onehot", [RT, RM, E], BF16)
        r0 = {n: sb(f"r0_{n}", [RT, RM]) for n in "top best total prob rank base over slotf tok".split()}
        slot = [sb(f"slot{i}", [RT, RM], I32) for i in range(2)]
        seen = sb("seen", [RT, E])
        pay = [sb(f"pay{i}", [RT, RM, ROW]) for i in range(2)]
        plain = [sb(f"plain{i}", [RT, RM, P]) for i in range(2)]
        turn = sb("turn", [1, 2])
        empty = sb("empty", [ET, EM, ROW])
        wexp = sb("wexp", [P, E, P])
        bexp = sb("bexp", [ET, E, P])
        rows = [sb(f"rows{i}", [ET, EM, ROW]) for i in range(2)]
        ut = sb("ut", [P, EM, ET])
        res = [sb(f"res{i}", [ET, EM, P]) for i in range(2)]
        where = [sb(f"where{i}", [ET, EM], I32) for i in range(2)]

        pair = [pb(f"pair{i}", 2) for i in range(4)]
        psH, psC, psV, psB, psY, psC2, psV2, psM = [p[:, i, :] for p in pair for i in range(2)]
        bk = [p[:, i, :] for p in pair for i in range(2)]
        near_ps, far_ps, route_ps = pair[1], pair[2], pair[3]

        names = """cst_in weights_in ssm_in_dma conv_w x0 x1 conv_done h0 cen1 sq1 var1 std1 rstd1 u1_ready bu vin_ready
            scan_done state_ready y1 dterm h1 cen2 sq2_ready var2 std2_ready rstd2_ready u2_ready msum_ready
            dve_setup tables eps_ready
            wb_in empty_ready turn_ready prefilled route_bf pads_ready gate_pe gate_dve gate_act pick_ready
            wsel0 wsel1 ffn_y ffn_done h2 cen3 sq3 var3 ln3 rstd3 u3_ready q_mm k_mm a_mm v_mm q_ready k_ready a_ready v_ready
            qs_ready lv1 lv2 lv4 lv8 lv16 lv32 lv64 lv128 upd masked near_placed far_placed cross_placed
            av den_ready rden_ready mixed_ready mixed_T h3
            cen4 sq4 var4 ln4 rstd4 u4_ready r_dve ranks_read r_shifted exps_ready onehot_ready prob_ready
            u4T hT pay_u pay_h slot_ready plain_ready plain_out0 plain_out1 sent0 sent1
            rows0 rows1 rowsT ut_ready expert_y res_mm res_ready where_ready done0 done1""".split()
        s = {n: sem(n) for n in names}

        def units(eng, body, depth):
            peel = depth + depth % 2 + 2
            for u in range(peel):
                body(u, u % 2)
            with eng.Fori(peel // 2, U // 2) as k:
                body(2 * k, 0)
                body(2 * k + 1, 1)
            for u in range(U, U + depth):
                body(u, u % 2)

        def live(u, k=0):
            return not isinstance(u, int) or 0 <= u - k < U

        def need(eng, name, value):
            if not isinstance(value, int) or value > 0:
                eng.wait_ge(s[name], value)

        def dma_slot(eng, name, u, par):
            each = 16 * (RM if name == "sent" else 1)
            eng.wait_ge(s[f"{name}{par}"], u // 2 * each if isinstance(u, int) else (u - par) * (each // 2))

        def seg(t, u):
            return t[:, bass.ds(u * W, W)]

        def two(ap):
            return ap.rearrange("p (b t) -> p b t", b=BU)

        def near_at(n):
            bank, c = (0, n * P) if n < 2 else ((n + 1) % 2, 0)
            return near_ps[:, bank, c:c + P]

        block = ctx.enter_context(nc.Block())

        @block.sync
        def _(sp):
            sp.dma_start(wconv[:, :, :], ins["wconv2"]).then_inc(s["weights_in"], 16)
            sp.dma_start(wconv1[:, :, :], ins["wconv1"]).then_inc(s["weights_in"], 16)
            sp.dma_start(wconv0[:, :, :], ins["wconv0"]).then_inc(s["weights_in"], 16)
            sp.dma_start(cols[:, :], ins["cols"]).then_inc(s["weights_in"], 16)
            sp.dma_start(posb[:, :], ins["pos"]).then_inc(s["weights_in"], 16)

            def load_x(k, par):
                u = 2 * k + par
                need(sp, "conv_done", u - 1)
                sp.dma_start(xin[par][:, :, :], ins["x2"][:, bass.ds(u * BU, BU), :]).then_inc(s[f"x{par}"], 16)

            load_x(0, 0)
            sp.dma_start(cst[:, :], ins["cst"]).then_inc(s["cst_in"], 16)
            load_x(0, 1)
            for dst, name in ((wg, "wg"), (gate_b, "bg"), (be0, "be"), (bv, "bv"), (wswitch, "wswitch"),
                              (bswitch, "bswitch")):
                sp.dma_start(dst[:, :], ins[name]).then_inc(s["wb_in"], 16)
            sp.dma_start(wqkav[:, :, :], ins["wqkav"]).then_inc(s["wb_in"], 16)
            sp.dma_start(wexp[:, :, :], ins["wexp"]).then_inc(s["wb_in"], 16)
            sp.dma_start(bexp[:, :, :], ins["bexp"]).then_inc(s["wb_in"], 16)
            sp.dma_start(ssm_in[:, :], ins["ssm_in"]).then_inc(s["ssm_in_dma"], 16)
            sp.dma_start(ssm_out[:, :], ins["ssm_out"]).then_inc(s["ssm_in_dma"], 16)
            with sp.Fori(1, U // 2) as k:
                load_x(k, 0)
                load_x(k, 1)
            def load_expert(k, par):
                u = 2 * k + par
                need(sp, "ffn_y", u - 1)
                for b in range(BU):
                    e = sp.value_load(pick[0:1, bass.ds(u * BU + b, 1)], min_val=0, max_val=E - 1)
                    sp.dma_start(wsel[par][:, b, :], ins["we"][bass.ds(e, 1), :, :].rearrange("e d o -> (e d) o"))\
                      .then_inc(s[f"wsel{par}"], 16)

            def store_plain(k, par):
                u = 2 * k + par
                need(sp, "plain_ready", u + 1)
                sp.dma_start(out[bass.ds(u * W, W), :].rearrange("(m p) f -> p m f", p=RT), plain[par][:, :, :])\
                  .then_inc(s[f"plain_out{par}"], 16)

            sp.wait_ge(s["pick_ready"], 1)
            load_expert(0, 0)
            load_expert(0, 1)
            with sp.Fori(1, U // 2) as t:
                load_expert(t, 0)
                store_plain(t - 1, 0)
                load_expert(t, 1)
                store_plain(t - 1, 1)
            store_plain(U // 2 - 1, 0)
            store_plain(U // 2 - 1, 1)

            for par in range(2):
                sp.wait_ge(s[f"sent{par}"], 16 * RM * U // 2)
                sp.wait_ge(s[f"plain_out{par}"], 16 * U // 2)

            def load_rows(t, par):
                e = 2 * t + par
                need(sp, "res_ready", e - 1)
                need(sp, "where_ready", e - 1)
                sp.dma_start(rows[par][:, :, :], slots[bass.ds(e * REGION, REGION), :].rearrange("(p m) c -> p m c", m=EM))\
                  .then_inc(s[f"rows{par}"], 16)

            load_rows(0, 0)
            load_rows(0, 1)
            with sp.Fori(1, E // 2) as t:
                load_rows(t, 0)
                load_rows(t, 1)

        @block.gpsimd
        def _(pool):
            pool.memset(empty[:, :, :], 0.0).then_inc(s["empty_ready"], 1)
            pool.wait_ge(s["empty_ready"], 1)
            pool.memset(empty[:, :, ROW - 1:ROW], NOWHERE).then_inc(s["empty_ready"], 1)
            for t in q + k:
                pool.memset(t[:, :, L:LP], 0.0).then_inc(s["pads_ready"], 1)
            for t in a:
                pool.memset(t[:, :, L:LP], 1.0).then_inc(s["pads_ready"], 1)
            for t in v:
                pool.memset(t[:, :, P:P + 1], 1.0).then_inc(s["pads_ready"], 1)
            pool.memset(u3[:, :, L:LP], 0.0).then_inc(s["pads_ready"], 1)
            pool.memset(attn[:, :, :, :], 0.0).then_inc(s["pads_ready"], 1)
            pool.wait_ge(s["pads_ready"], PADS)
            pool.memset(turn[:, :], 0.0).then_inc(s["turn_ready"], 1)
            pool.wait_ge(s["turn_ready"], 1)

            def gate_dmas(n):
                need(pool, "turn_ready", n + 1)
                pool.tensor_tensor(turn[:, 0:1], turn[:, 1:2], turn[:, 1:2], ALU.add).then_inc(s["turn_ready"], 1)

            def body(u, par):
                y = u - 2
                if live(y):
                    need(pool, "slot_ready", y + 1)
                    need(pool, "plain_ready", y + 1)
                    gate_dmas(y)
                    for m in range(RM):
                        pool.indirect_dma_start(
                            out=slots, out_offset=bass.IndirectOffsetOnAxis(ap=slot[par][:, m:m + 1], axis=0),
                            in_=pay[par][:, m, :], in_offset=None, bounds_check=E * REGION - 1, oob_is_err=False)\
                            .then_inc(s[f"sent{par}"], 16)

            pool.wait_ge(s["prefilled"], 16 * E)
            units(pool, body, 2)

            def scatter(t, par):
                e = 2 * t + par
                need(pool, "res_ready", e + 1)
                need(pool, "where_ready", e + 1)
                gate_dmas(U + e)
                for m in range(EM):
                    pool.indirect_dma_start(
                        out=out, out_offset=bass.IndirectOffsetOnAxis(ap=where[par][:, m:m + 1], axis=0),
                        in_=res[par][:, m, :], in_offset=None, bounds_check=NTOK - 1, oob_is_err=False)\
                        .then_inc(s[f"done{par}"], 16)

            for par in range(2):
                pool.wait_ge(s[f"plain_out{par}"], 16 * U // 2)
            with pool.Fori(0, E // 2) as t:
                scatter(t, 0)
                scatter(t, 1)
            for par in range(2):
                pool.wait_ge(s[f"done{par}"], 16 * EM * E // 2)

        @block.tensor
        def _(pe):
            pe.wait_ge(s["conv_w"], 1)

            def x_wait(u, par):
                if isinstance(u, int):
                    pe.wait_ge(s[f"x{par}"], 16 * (u // 2 + 1))
                else:
                    pe.wait_ge(s[f"x{par}"], (u - par) * 8 + 16)

            def conv(u, par, a, b):
                for j in range(a, b):
                    mm = pe.matmul(psH[:, 0:W], wconv[:, j, :], xin[par][:, :, 2 * j:2 * j + L],
                                   start=(j == 0), stop=(j == TAPS - 1))
                if b == TAPS:
                    mm.then_inc(s["conv_done"], 1)

            def body(u, par):
                v, y = u - 1, u - 2
                if live(y):
                    need(pe, "state_ready", y + 1)
                    need(pe, "h1", y)
                    pe.matmul(psY[:, 0:W], ssm_out[:, :], state[:, :], start=True, stop=True).then_inc(s["y1"], 1)
                if live(u):
                    x_wait(u, par)
                    need(pe, "h0", u)
                    conv(u, par, 0, 2)
                if live(v):
                    need(pe, "h0", v + 1)
                    need(pe, "u1_ready", v)
                    pe.matmul(psC[:, 0:W], const("center"), seg(h, v), start=True, stop=True).then_inc(s["cen1"], 1)
                if live(y):
                    need(pe, "h1", y + 1)
                    need(pe, "u2_ready", y)
                    pe.matmul(psC2[:, 0:W], const("center"), seg(h, y), start=True, stop=True).then_inc(s["cen2"], 1)
                if live(u):
                    conv(u, par, 2, 4)
                if live(v):
                    need(pe, "sq1", v + 1)
                    need(pe, "std1", v)
                    pe.matmul(psV[:, 0:W], const("mean"), sq[:, :], start=True, stop=True).then_inc(s["var1"], 1)
                if live(y):
                    need(pe, "sq2_ready", y + 1)
                    need(pe, "std2_ready", y)
                    pe.matmul(psV2[:, 0:W], const("mean"), sq2[:, :], start=True, stop=True).then_inc(s["var2"], 1)
                if live(u):
                    conv(u, par, 4, 6)
                if live(v):
                    need(pe, "u1_ready", v + 1)
                    need(pe, "vin_ready", v)
                    pe.matmul(psB[:, 0:W], ssm_in[:, :], u1[:, :], start=True, stop=True).then_inc(s["bu"], 1)
                if live(u):
                    conv(u, par, 6, 8)

            pe.wait_ge(s["cst_in"], 16)
            pe.wait_ge(s["ssm_in_dma"], 32)
            units(pe, body, 2)

            gps = bk[0]
            pe.wait_ge(s["wb_in"], WB_IN)
            pe.wait_ge(s["msum_ready"], U)
            pe.wait_ge(s["h0"], U)
            pe.wait_ge(s["vin_ready"], U)
            pe.wait_ge(s["h1"], U)
            pe.matmul(gps[0:B, 0:E], msum[:, :], wg[:, :], start=True, stop=True).then_inc(s["gate_pe"], 1)
            pe.wait_ge(s["gate_dve"], 2)
            pe.matmul(bk[1][0:E, 0:B], gs[:, 3 * E:4 * E], const("ident")[0:B, 0:B], start=True, stop=True)
            pe.matmul(bk[2][0:1, 0:B], pick_f[:, :], const("ident")[0:B, 0:B], start=True, stop=True)\
              .then_inc(s["gate_pe"], 1)
            pe.wait_ge(s["gate_dve"], 3)
            pe.matmul(bk[3][:, 0:B], const("ones")[0:E, :], gT[:, :], start=True, stop=True)
            pe.matmul(bk[4][:, 0:B], be0[:, :], gT[:, :], start=True, stop=True).then_inc(s["gate_pe"], 1)
            pe.wait_ge(s["gate_dve"], 4)
            pe.wait_ge(s["pads_ready"], PADS)
            pe.wait_ge(s["route_bf"], 2)

            def near_level(n, kk, qq):
                for m in range(NT):
                    for g in range(4):
                        at = m * TILE + 32 * g
                        mm = pe.matmul(near_at(n)[32 * g:32 * g + 32, m * 32:m * 32 + 32],
                                       kk[:, at:at + 32], qq[:, at:at + 32], start=True, stop=True)
                return mm

            def far_level(kk, size):
                for m in range(NT):
                    for at in range(0, TILE, 2 * size):
                        c = m * TILE + at
                        mm = pe.matmul(far_ps[at:at + size, 0, c + size:c + 2 * size], kk[:, c:c + size],
                                       qs[:, c + size:c + 2 * size], start=True, stop=True)
                return mm

            def body(u, par):
                v_, y = u - 1, u - 2
                vp = 1 - par
                kf = k[vp][:, :, :].rearrange("p b t -> p (b t)")
                qf = q[vp][:, :, :].rearrange("p b t -> p (b t)")
                if live(v_):
                    need(pe, "qs_ready", v_ + 1)
                    need(pe, "k_ready", v_ + 1)
                    need(pe, "q_ready", v_ + 1)
                    need(pe, "mixed_ready", v_)
                    near_level(0, kf, qf)
                    near_level(1, kf, qs).then_inc(s["lv1"], 1)
                if live(u):
                    if isinstance(u, int):
                        pe.wait_ge(s[f"wsel{par}"], 32 * (u // 2 + 1))
                    else:
                        pe.wait_ge(s[f"wsel{par}"], (u - par) * 16 + 32)
                    need(pe, "a_ready", u)
                    for b in range(BU):
                        mm = pe.matmul(bk[0][:, b * L:(b + 1) * L], wsel[par][:, b, :],
                                       u2[:, bass.ds(u * W + b * L, L)], start=True, stop=True)
                    mm.then_inc(s["ffn_y"], 1)
                for n, size in enumerate((2, 4, 8, 16)):
                    if live(v_):
                        need(pe, "upd", v_ * 7 + n + 1)
                        if n > 0:
                            need(pe, "masked", v_ * 6 + n + 1)
                        near_level(n + 2, kf, qs).then_inc(s[f"lv{size}"], 1)
                    if size == 2 and live(y):
                        need(pe, "h3", y + 1)
                        need(pe, "plain_ready", y)
                        pe.matmul(bk[6][:, 0:W], const("center"), h3[par][:, :], start=True, stop=True).then_inc(s["cen4"], 1)
                    if size == 4 and live(u):
                        need(pe, "h2", u + 1)
                        need(pe, "v_ready", u)
                        pe.matmul(bk[1][:, 0:W], const("center"), seg(h, u), start=True, stop=True).then_inc(s["cen3"], 1)
                    if size == 8 and live(y):
                        need(pe, "sq4", y + 1)
                        pe.matmul(bk[7][:, 0:W], const("mean"), sq2[:, :], start=True, stop=True).then_inc(s["var4"], 1)
                    if size == 16 and live(u):
                        need(pe, "sq3", u + 1)
                        need(pe, "ffn_done", u + 1)
                        pe.matmul(bk[0][:, 0:W], const("mean"), sq[:, :], start=True, stop=True).then_inc(s["var3"], 1)
                if live(v_):
                    need(pe, "upd", v_ * 7 + 5)
                    need(pe, "h3", v_)
                    far_level(kf, 32).then_inc(s["lv32"], 1)
                if live(y):
                    need(pe, "u4_ready", y + 1)
                    need(pe, "ln4", y + 1)
                    for m in range(RM):
                        mm = pe.matmul(bk[7][0:RT, m * E:(m + 1) * E], u4[:, m * RT:(m + 1) * RT], wswitch[:, :],
                                       start=True, stop=True)
                    for m in range(RM):
                        dst = bk[6][0:RT, m * P:(m + 1) * P] if m < 4 else bk[7][0:RT, 384:512]
                        mm = pe.transpose(dst, u4[:, m * RT:(m + 1) * RT], const("ident"))
                    mm.then_inc(s["u4T"], 1)
                if live(v_):
                    need(pe, "upd", v_ * 7 + 6)
                    far_level(kf, 64).then_inc(s["lv64"], 1)
                if live(u):
                    need(pe, "u3_ready", u + 1)
                    need(pe, "ln3", u + 1)
                    pe.matmul(two(bk[0][:, 0:W]), wqkav[:, 0, :], u3[:, :, 0:L], start=True, stop=True).then_inc(s["q_mm"], 1)
                    pe.matmul(two(bk[1][:, 0:W]), wqkav[:, 1, :], u3[:, :, 0:L], start=True, stop=True).then_inc(s["k_mm"], 1)
                if live(v_):
                    need(pe, "upd", v_ * 7 + 7)
                    for b in range(BU):
                        mm = pe.matmul(far_ps[:, 1, b * P:(b + 1) * P], kf[:, b * LP:b * LP + TILE],
                                       qs[:, b * LP + TILE:(b + 1) * LP], start=True, stop=True)
                    mm.then_inc(s["lv128"], 1)
                if live(u):
                    need(pe, "q_ready", u + 1)
                    pe.matmul(two(bk[0][:, 0:W]), wqkav[:, 2, :], u3[:, :, 0:L], start=True, stop=True).then_inc(s["a_mm"], 1)
                    need(pe, "k_ready", u + 1)
                    for m in range(NT):
                        mm = pe.matmul(bk[1][:, m * P:(m + 1) * P], u3[:, m // TPB, (m % TPB) * TILE:(m % TPB + 1) * TILE],
                                       wqkav[:, 3, :], start=True, stop=True)
                    mm.then_inc(s["v_mm"], 1)
                if live(y):
                    need(pe, "onehot_ready", y + 1)
                    need(pe, "pay_u", y * RM + RM)
                    oh = onehot[:, :, :].rearrange("p m e -> p (m e)")
                    pe.matmul(bk[7][0:RT, 96:96 + RM * E], upper_bf[:, :], oh[:, 0:RM * E], start=True, stop=False,
                              skip_group_check=True)
                    for d in range(1, RM + 1):
                        mm = pe.matmul(bk[7][0:RT, 96 + d * E:96 + (RM + 1) * E], ones_bf[:, :], oh[:, 0:(RM + 1 - d) * E],
                                       start=False, stop=(d == RM), skip_group_check=True)
                    for m in range(RM):
                        dst = bk[6][0:RT, m * P:(m + 1) * P] if m < 4 else bk[7][0:RT, 384:512]
                        mm = pe.transpose(dst, h3[par][:, m * RT:(m + 1) * RT], const("ident"))
                    mm.then_inc(s["hT"], 1)
                if live(v_):
                    need(pe, "near_placed", v_ * 4 + 4)
                    need(pe, "far_placed", v_ * 3 + 3)
                    need(pe, "cross_placed", v_ + 1)
                    need(pe, "v_ready", v_ + 1)
                    for b in range(BU):
                        pe.matmul(near_ps[:, b, 0:P + 1], attn[:, b, 0, :], v[vp][:, b * TPB, :], start=True, stop=True)
                        pe.matmul(near_ps[:, b, P + 1:2 * P + 2], attn[:, b, 1, :], v[vp][:, b * TPB, :],
                                  start=True, stop=False)
                        mm = pe.matmul(near_ps[:, b, P + 1:2 * P + 2], attn[:, b, 2, :], v[vp][:, b * TPB + 1, :],
                                       start=False, stop=True)
                    mm.then_inc(s["av"], 1)
                    need(pe, "mixed_ready", v_ + 1)
                    for m in range(NT):
                        b, second = m // TPB, m % TPB
                        n = L - TILE if second else TILE
                        c = b * L + second * TILE
                        mm = pe.transpose(far_ps[:, 0, c:c + n], mixed[0:n, m, :], const("ident")[0:n, 0:n])
                    mm.then_inc(s["mixed_T"], 1)

            units(pe, body, 2)

            pe.wait_ge(s["plain_ready"], U)
            pe.wait_ge(s["h3"], U)

            def expert(t, par):
                e = 2 * t + par
                if isinstance(t, int):
                    pe.wait_ge(s[f"rows{par}"], 16 * (t + 1))
                else:
                    pe.wait_ge(s[f"rows{par}"], t * 16 + 16)
                need(pe, "ut_ready", e)
                for m in range(EM):
                    mm = pe.transpose(pair[0][:, m // 4, (m % 4) * ET:(m % 4 + 1) * ET], rows[par][:, m, 0:P],
                                      const("ident")[0:ET, 0:ET])
                mm.then_inc(s["rowsT"], 1)
                need(pe, "ut_ready", e + 1)
                need(pe, "res_mm", e)
                for m in range(EM):
                    mm = pe.matmul(pair[1][0:ET, m // 4, (m % 4) * P:(m % 4 + 1) * P], ut[:, m, :],
                                   wexp[:, bass.ds(e, 1), :].rearrange("p e f -> p (e f)"), start=True, stop=True)
                mm.then_inc(s["expert_y"], 1)

            expert(0, 0)
            expert(0, 1)
            with pe.Fori(1, E // 2) as t:
                expert(t, 0)
                expert(t, 1)

        @block.scalar
        def _(act):
            def body(u, par):
                v, y = u - 1, u - 2
                if live(v):
                    need(act, "cen1", v + 1)
                    need(act, "var1", v)
                    act.activation(sq[:, :], psC[:, 0:W], ACT.Square).then_inc(s["sq1"], 1)
                if live(y):
                    need(act, "cen2", y + 1)
                    need(act, "var2", y)
                    act.activation(sq2[:, :], psC2[:, 0:W], ACT.Square).then_inc(s["sq2_ready"], 1)
                if live(v):
                    need(act, "var1", v + 1)
                    need(act, "rstd1", v)
                    act.activation(std[:, :], psV[:, 0:W], ACT.Ln, bias=eps[:, :]).then_inc(s["std1"], 1)
                    need(act, "std1", v + 1)
                    need(act, "u1_ready", v)
                    act.activation(rstd[:, :], std[:, :], ACT.Exp, scale=-0.5).then_inc(s["rstd1"], 1)
                if live(y):
                    need(act, "var2", y + 1)
                    need(act, "rstd2_ready", y)
                    act.activation(std2[:, :], psV2[:, 0:W], ACT.Ln, bias=eps[:, :]).then_inc(s["std2_ready"], 1)
                    need(act, "std2_ready", y + 1)
                    need(act, "u2_ready", y)
                    act.activation(rstd2[:, :], std2[:, :], ACT.Exp, scale=-0.5).then_inc(s["rstd2_ready"], 1)

            act.wait_ge(s["empty_ready"], 2)
            for e in range(E):
                act.dma_start(slots[e * REGION:(e + 1) * REGION, :].rearrange("(p m) c -> p m c", m=EM), empty[:, :, :])\
                   .then_inc(s["prefilled"], 16)
            act.wait_ge(s["eps_ready"], 1)
            act.wait_ge(s["tables"], 1)
            act.activation(tab[:, 12:13], tab[:, 11:12], ACT.Sqrt).then_inc(s["tables"], 1)
            act.preload_act_table_set(LN_EXP)
            units(act, body, 2)

            act.wait_ge(s["gate_dve"], 1)
            act.activation(gs[:, 2 * E:3 * E], gs[:, E:2 * E], ACT.Exp).then_inc(s["gate_act"], 1)
            act.wait_ge(s["gate_dve"], 4)
            act.wait_ge(s["pads_ready"], PADS)

            def body(u, par):
                v_, y = u - 1, u - 2
                if live(u):
                    need(act, "ffn_y", u + 1)
                    need(act, "h2", u)
                    for b in range(BU):
                        at = bass.ds(u * BU + b, 1)
                        f = act.activation(ffn[:, b * L:(b + 1) * L], bk[0][:, b * L:(b + 1) * L], ACT.Identity,
                                           bias=gbias[:, at], scale=gate[:, at])
                    f.then_inc(s["ffn_done"], 1)
                if live(y):
                    need(act, "cen4", y + 1)
                    need(act, "var4", y)
                    act.activation(sq2[:, :], bk[6][:, 0:W], ACT.Square).then_inc(s["sq4"], 1)
                if live(u):
                    need(act, "cen3", u + 1)
                    need(act, "var3", u)
                    act.activation(sq[:, :], bk[1][:, 0:W], ACT.Square).then_inc(s["sq3"], 1)
                act.preload_act_table_set(LN_EXP)
                if live(y):
                    need(act, "var4", y + 1)
                    act.activation(std2[:, :], bk[7][:, 0:W], ACT.Ln, bias=eps[:, :]).then_inc(s["ln4"], 1)
                    need(act, "ln4", y + 1)
                    need(act, "u4_ready", y)
                    act.activation(rstd2[:, :], std2[:, :], ACT.Exp, scale=-0.5).then_inc(s["rstd4"], 1)
                if live(u):
                    need(act, "var3", u + 1)
                    act.activation(std[:, :], bk[0][:, 0:W], ACT.Ln, bias=eps[:, :]).then_inc(s["ln3"], 1)
                    need(act, "ln3", u + 1)
                    need(act, "u3_ready", u)
                    act.activation(rstd[:, :], std[:, :], ACT.Exp, scale=-0.5).then_inc(s["rstd3"], 1)
                if live(y):
                    need(act, "r_shifted", y + 1)
                    act.activation(r1["exps"][:, :, :], r1["shifted"][:, :, :], ACT.Exp).then_inc(s["exps_ready"], 1)
                if live(v_):
                    need(act, "av", v_)
                    need(act, "lv64", v_ + 1)
                    need(act, "masked", v_ * 6 + 6)
                    for g in range(4):
                        act.copy(attn[32 * g:32 * g + 32, :, 0:3:2, 32 * g:32 * g + 32],
                                 near[32 * g:32 * g + 32, :, :].rearrange("p (b t) c -> p b t c", b=BU))\
                           .then_inc(s["near_placed"], 1)
                    for lo, n in ((0, 32), (64, 32), (0, 64)):
                        act.copy(attn[lo:lo + n, :, 0:3:2, lo + n:lo + 2 * n],
                                 far_ps[lo:lo + n, 0, :].rearrange("p (b t c) -> p b t c", b=BU, t=TPB)
                                 [:, :, :, lo + n:lo + 2 * n]).then_inc(s["far_placed"], 1)
                if live(u):
                    need(act, "q_mm", u + 1)
                    act.activation(q[par][:, :, 0:L], two(bk[0][:, 0:W]), ACT.Relu, bias=cols[:, 6:7]).then_inc(s["q_ready"], 1)
                    need(act, "k_mm", u + 1)
                    act.activation(k[par][:, :, 0:L], two(bk[1][:, 0:W]), ACT.Relu, bias=cols[:, 7:8]).then_inc(s["k_ready"], 1)
                if live(v_):
                    need(act, "lv128", v_ + 1)
                    act.copy(attn[:, :, 1, :], far_ps[:, 1, 0:BU * P].rearrange("p (b c) -> p b c", b=BU))\
                       .then_inc(s["cross_placed"], 1)
                if live(y):
                    need(act, "u4T", y + 1)
                    need(act, "prob_ready", y + 1)
                    if live(y, 2):
                        dma_slot(act, "sent", y, par)
                    for m in range(RM):
                        src = bk[6][0:RT, m * P:(m + 1) * P] if m < 4 else bk[7][0:RT, 384:512]
                        act.activation(pay[par][:, m, 0:P], src, ACT.Copy, scale=r0["prob"][:, m:m + 1])\
                           .then_inc(s["pay_u"], 1)
                if live(u):
                    need(act, "a_mm", u + 1)
                    act.activation(a[par][:, :, 0:L], two(bk[0][:, 0:W]), ACT.Sigmoid, bias=cols[:, 8:9]).then_inc(s["a_ready"], 1)
                if live(y):
                    need(act, "hT", y + 1)
                    act.copy(pay[par][:, 0:4, P:2 * P], bk[6][0:RT, :].rearrange("p (m f) -> p m f", m=4))\
                       .then_inc(s["pay_h"], 1)
                    need(act, "ranks_read", y + 1)
                    act.copy(pay[par][:, 4, P:2 * P], bk[7][0:RT, 384:512]).then_inc(s["pay_h"], 1)

            units(act, body, 2)

            def turn_rows(t, par):
                e = 2 * t + par
                need(act, "rowsT", e + 1)
                need(act, "expert_y", e)
                act.copy(ut[:, 0:4, :], pair[0][:, 0, 0:4 * ET].rearrange("p (m r) -> p m r", m=4))
                act.copy(ut[:, 4, :], pair[0][:, 1, 0:ET]).then_inc(s["ut_ready"], 1)

            turn_rows(0, 0)
            turn_rows(0, 1)
            with act.Fori(1, E // 2) as t:
                turn_rows(t, 0)
                turn_rows(t, 1)
        @block.vector
        def _(dve):
            steps = [0]

            def then(ins):
                steps[0] += 1
                ins.then_inc(s["dve_setup"], 1)
                dve.wait_ge(s["dve_setup"], steps[0])

            dve.memset(eps[:, :], LN_EPS).then_inc(s["eps_ready"], 1)
            dve.wait_ge(s["weights_in"], 80)
            n1 = TAPS // 2 * P
            wc = wconv[:, :, :].rearrange("p j h -> p (j h)")
            then(dve.tensor_tensor(wc[:, 0:n1], wc[:, 0:n1], wconv1[:, :, :].rearrange("p j h -> p (j h)"), ALU.add))
            dve.tensor_tensor(wc[:, 0:n1 // 2], wc[:, 0:n1 // 2], wconv0[:, :, :].rearrange("p j h -> p (j h)"),
                              ALU.add).then_inc(s["conv_w"], 1)
            c_b0, c_ar, c_ai, c_dv = 0, 3, 4, 5
            t = lambda i: tab[:, i:i + 1]
            tt, ts, stt = dve.tensor_tensor, dve.tensor_scalar, dve.scalar_tensor_tensor
            then(dve.tensor_reduce(t(0), cols[:, 0:3], AX_X, ALU.add))
            then(ts(t(0), t(0), 1.0 / 3.0, None, ALU.mult))
            then(ts(posb[:, :], posb[:, :], t(0), None, ALU.add))

            then(ts(t(0), cols[:, c_ar:c_ar + 1], -1.0, None, ALU.mult))
            then(tt(t(0), t(0), cols[:, c_ar:c_ar + 1], ALU.min))
            then(ts(t(0), t(0), -DAMP_MIN, None, ALU.add))
            then(ts(t(1), t(0), DT / 2, None, ALU.mult))
            then(ts(t(2), cols[:, c_ai:c_ai + 1], DT / 2, None, ALU.mult))
            then(ts(t(3), t(1), -1.0, 1.0, ALU.mult, ALU.add))
            then(tt(t(4), t(2), t(2), ALU.mult))
            then(stt(t(4), t(3), t(3), t(4), ALU.mult, ALU.add))
            then(dve.reciprocal(t(4), t(4)))
            then(tt(t(5), t(3), t(4), ALU.mult))
            then(tt(t(6), t(2), t(4), ALU.mult))
            then(ts(t(3), t(1), 1.0, None, ALU.add))
            then(tt(t(7), t(2), t(6), ALU.mult))
            then(stt(t(8), t(3), t(5), t(7), ALU.mult, ALU.subtract))
            then(tt(t(7), t(2), t(5), ALU.mult))
            then(stt(t(9), t(3), t(6), t(7), ALU.mult, ALU.add))
            then(tt(t(7), t(9), t(9), ALU.mult))
            then(stt(t(10), t(8), t(8), t(7), ALU.mult, ALU.add))
            ts(t(11), t(10), 1e-30, None, ALU.max).then_inc(s["tables"], 1)
            dve.wait_ge(s["tables"], 2)
            then(dve.reciprocal(t(13), t(12)))
            then(stt(t(13), t(11), t(13), t(12), ALU.mult, ALU.add))
            then(ts(t(12), t(13), 0.5, None, ALU.mult))
            then(dve.reciprocal(t(13), t(12)))
            then(ts(t(14), t(10), 0.0, None, ALU.is_equal))
            then(tt(t(15), t(8), t(13), ALU.mult))
            then(tt(t(15), t(15), t(14), ALU.add))
            then(tt(t(16), t(9), t(13), ALU.mult))
            dve.memset(decay[:, :, :], 0.0)
            then(ts(t(5), t(5), DT, None, ALU.mult))
            then(ts(t(6), t(6), DT, None, ALU.mult))
            dve.memset(cosn[:, 0:1], 1.0)
            then(dve.memset(sinn[:, 0:1], 0.0))
            n = 1
            while n < L:
                then(ts(tmpn[:, 0:n], sinn[:, 0:n], t(16), None, ALU.mult))
                stt(cosn[:, n:2 * n], cosn[:, 0:n], t(15), tmpn[:, 0:n], ALU.mult, ALU.subtract)
                then(ts(tmpn[:, n:2 * n], cosn[:, 0:n], t(16), None, ALU.mult))
                then(stt(sinn[:, n:2 * n], sinn[:, 0:n], t(15), tmpn[:, n:2 * n], ALU.mult, ALU.add))
                then(tt(t(17), t(16), t(16), ALU.mult))
                then(stt(t(18), t(15), 2.0, t(16), ALU.mult, ALU.mult))
                then(stt(t(15), t(15), t(15), t(17), ALU.mult, ALU.subtract))
                then(dve.tensor_copy(t(16), t(18)))
                n *= 2
            top, low = slice(0, N_STATE), slice(N_STATE, P)
            then(ts(tmpn[top, 0:L], sinn[top, 0:L], tab[top, 6:7], None, ALU.mult))
            then(stt(tin[top, :], cosn[top, 0:L], tab[top, 5:6], tmpn[top, 0:L], ALU.mult, ALU.add))
            then(ts(tmpn[low, 0:L], sinn[low, 0:L], tab[low, 5:6], None, ALU.mult))
            then(stt(tin[low, :], cosn[low, 0:L], tab[low, 6:7], tmpn[low, 0:L], ALU.mult, ALU.subtract))
            then(dve.tensor_copy(tout[top, :], cosn[top, 0:L]))
            then(ts(tout[low, :], sinn[low, 0:L], -1.0, None, ALU.mult))
            for b in range(BU):
                then(ts(decay[:, b, 1:L], cosn[:, 1:L], 0.0, t(12), ALU.mult, ALU.add))

            dve.wait_ge(s["cst_in"], 16)
            dve.tensor_copy(upper_bf[:, :], const("upper")[0:RT, 0:RT]).then_inc(s["route_bf"], 1)
            dve.memset(ones_bf[:, :], 1.0).then_inc(s["route_bf"], 1)

            def over_batches(ap):
                return ap.rearrange("p (a t) -> p a t", a=1).to_broadcast([P, BU, L])

            def body(u, par):
                v, y = u - 1, u - 2
                if live(y):
                    need(dve, "y1", y + 1)
                    need(dve, "dterm", y + 1)
                    dve.tensor_tensor(seg(h, y), seg(h, y), psY[:, 0:W], ALU.add).then_inc(s["h1"], 1)
                if live(v):
                    need(dve, "rstd1", v + 1)
                    need(dve, "bu", v)
                    need(dve, "dterm", v)
                    dve.tensor_tensor(u1[:, :], psC[:, 0:W], rstd[:, :], ALU.mult).then_inc(s["u1_ready"], 1)
                if live(v):
                    need(dve, "bu", v + 1)
                    need(dve, "scan_done", v)
                    dve.tensor_tensor(two(vin[:, :]), two(psB[:, 0:W]), over_batches(tin[:, :]),
                                      ALU.mult).then_inc(s["vin_ready"], 1)
                if live(y):
                    need(dve, "rstd2_ready", y + 1)
                    dve.tensor_tensor(seg(u2, y), psC2[:, 0:W], rstd2[:, :], ALU.mult).then_inc(s["u2_ready"], 1)
                if live(v):
                    need(dve, "vin_ready", v + 1)
                    need(dve, "state_ready", v)
                    need(dve, "y1", v)
                    dve.tensor_tensor_scan(state[:, :], decay[:, :, :].rearrange("p b t -> p (b t)"), vin[:, :], 0.0,
                                           ALU.mult, ALU.add).then_inc(s["scan_done"], 1)
                    need(dve, "u1_ready", v + 1)
                    dve.scalar_tensor_tensor(seg(h, v), u1[:, :], cols[:, 5:6], seg(h, v), ALU.mult,
                                             ALU.add).then_inc(s["dterm"], 1)
                if live(y):
                    need(dve, "u2_ready", y + 1)
                    dve.tensor_reduce(msum[:, bass.ds(y * BU, BU)], two(seg(u2, y)), AX_X, ALU.add)\
                       .then_inc(s["msum_ready"], 1)
                if live(v):
                    need(dve, "scan_done", v + 1)
                    dve.tensor_tensor(two(state[:, :]), two(state[:, :]), over_batches(tout[:, :]),
                                      ALU.mult).then_inc(s["state_ready"], 1)
                if live(u):
                    need(dve, "conv_done", u + 1)
                    dve.scalar_tensor_tensor(two(seg(h, u)), two(psH[:, 0:W]), 1.0 / 3.0, over_batches(posb[:, :]),
                                             ALU.mult, ALU.add).then_inc(s["h0"], 1)

            units(dve, body, 2)

            def chain(ins, name):
                ins.then_inc(s[name], 1)

            g = lambda i: gs[:, i * E:(i + 1) * E]
            g1 = lambda i: gs[:, 7 * E + i:7 * E + i + 1]
            dve.wait_ge(s["wb_in"], WB_IN)
            dve.wait_ge(s["gate_pe"], 1)
            then(stt(g(0), bk[0][0:B, 0:E], 1.0 / L, gate_b[:, :], ALU.mult, ALU.add))
            then(dve.tensor_reduce(g1(0), g(0), AX_X, ALU.max))
            ts(g(1), g(0), g1(0), None, ALU.subtract).then_inc(s["gate_dve"], 1)
            then(ts(g(4), g(0), g1(0), None, ALU.is_equal))
            then(tt(g(4), g(4), const("first_wins")[0:B, :], ALU.mult))
            then(dve.tensor_reduce(g1(1), g(4), AX_X, ALU.max))
            then(ts(g(4), g(4), g1(1), None, ALU.is_equal))
            dve.wait_ge(s["gate_act"], 1)
            then(dve.tensor_reduce(g1(2), g(2), AX_X, ALU.add))
            then(dve.reciprocal(g1(3), g1(2)))
            then(ts(g(3), g(4), g1(3), None, ALU.mult))
            then(tt(g(5), g(4), const("expert_id")[0:B, :], ALU.mult))
            dve.tensor_reduce(pick_f[:, :], g(5), AX_X, ALU.add).then_inc(s["gate_dve"], 1)
            dve.wait_ge(s["gate_pe"], 2)
            dve.tensor_copy(pick[:, :], bk[2][0:1, 0:B]).then_inc(s["pick_ready"], 1)
            dve.tensor_copy(gT[:, :], bk[1][0:E, 0:B]).then_inc(s["gate_dve"], 1)
            dve.wait_ge(s["gate_pe"], 3)
            then(dve.tensor_copy(gate[:, :], bk[3][:, 0:B]))
            dve.tensor_copy(gbias[:, :], bk[4][:, 0:B]).then_inc(s["gate_dve"], 1)
            then(dve.memset(seen[:, :], 0.0))
            then(dve.tensor_copy(r0["tok"][:, :], const("token")[0:RT, :]))
            dve.wait_ge(s["gate_dve"], 4)
            dve.wait_ge(s["pads_ready"], PADS)

            def halves(ap, size):
                x = ap.rearrange("p (n two c) -> p n two c", two=2, c=size)
                return x[:, :, 0, :], x[:, :, 1, :]

            def route(ap):
                return ap.rearrange("p (m o) -> p m o", o=1).to_broadcast([RT, RM, E])

            def per_expert(ap):
                return ap.rearrange("p (o e) -> p o e", o=1).to_broadcast([RT, RM, E])

            def body(u, par):
                v_, y = u - 1, u - 2
                vp = 1 - par
                kf = k[vp][:, :, :].rearrange("p b t -> p (b t)")
                qf = q[vp][:, :, :].rearrange("p b t -> p (b t)")
                af = a[vp][:, :, :].rearrange("p b t -> p (b t)")

                def grow(size, n):
                    block = af if size == 1 else prod[size][:, :]
                    tl, tr = halves(block, 1)
                    ql, qr = halves(qs[:, :], size)
                    kl, kr = halves(kf, size)
                    shape = [P, BU * LP // (2 * size), size]
                    if size <= 16:
                        need(dve, "masked", v_ * 6 + {1: 1, 2: 2, 4: 3, 8: 4, 16: 5}[size])
                    if size == 1:
                        need(dve, "lv1", v_ + 1)
                    else:
                        need(dve, f"lv{size}", v_ + 1)
                        need(dve, "upd", v_ * 7 + n)
                    if size < 64:
                        tt(prod[2 * size][:, :], tl[:, :, 0], tr[:, :, 0], ALU.mult)
                    tt(qr, qr, tl.to_broadcast(shape), ALU.mult)
                    tt(kl, kl, tr.to_broadcast(shape), ALU.mult).then_inc(s["upd"], 1)

                def mask(n, size):
                    src = near_at(n).rearrange("p (m c) -> p m c", m=NT)
                    if n == 0:
                        need(dve, "lv1", v_ + 1)
                        need(dve, "near_placed", v_ * 4)
                        m = const("diag32").rearrange("p (o c) -> p o c", o=1).to_broadcast([P, NT, 32])
                        tt(near[:, :, :], src, m, ALU.mult).then_inc(s["masked"], 1)
                    else:
                        m = const(f"level{size}").bitcast(I32).rearrange("p (o c) -> p o c", o=1).to_broadcast([P, NT, 32])
                        dve.copy_predicated(near[:, :, :], m, src).then_inc(s["masked"], 1)

                if live(v_):
                    need(dve, "q_ready", v_ + 1)
                    need(dve, "a_ready", v_ + 1)
                    need(dve, "lv128", v_)
                    tt(qs[:, :], qf, af, ALU.mult).then_inc(s["qs_ready"], 1)
                    need(dve, "k_ready", v_ + 1)
                    need(dve, "qs_ready", v_ + 1)
                    mask(0, 0)
                    grow(1, 0)
                    mask(1, 1)
                if live(u):
                    need(dve, "ffn_done", u + 1)
                    tt(seg(h, u), seg(h, u), ffn[:, :], ALU.add).then_inc(s["h2"], 1)
                if live(v_):
                    grow(2, 1)
                    mask(2, 2)
                    grow(4, 2)
                    mask(3, 4)
                    grow(8, 3)
                    mask(4, 8)
                if live(y):
                    need(dve, "rstd4", y + 1)
                    need(dve, "u4T", y)
                    tt(u4[:, :], bk[6][:, 0:W], rstd2[:, :], ALU.mult).then_inc(s["u4_ready"], 1)
                if live(v_):
                    grow(16, 4)
                    mask(5, 16)
                if live(u):
                    need(dve, "rstd3", u + 1)
                    need(dve, "v_mm", u)
                    tt(u3[:, :, 0:L], two(bk[1][:, 0:W]), two(rstd[:, :]), ALU.mult).then_inc(s["u3_ready"], 1)
                if live(v_):
                    grow(32, 5)
                if live(y):
                    r = r1
                    need(dve, "u4T", y + 1)
                    n = [0]

                    def step(ins):
                        n[0] += 1
                        ins.then_inc(s["r_dve"], 1)
                        dve.wait_ge(s["r_dve"], y * R_STEPS + n[0])

                    step(tt(r["logit"][:, :, :], bk[7][0:RT, 0:RM * E].rearrange("p (m e) -> p m e", m=RM),
                            per_expert(bswitch[:, :]), ALU.add))
                    step(dve.tensor_reduce(r0["top"][:, :], r["logit"][:, :, :], AX_X, ALU.max))
                    need(dve, "exps_ready", y)
                    tt(r["shifted"][:, :, :], r["logit"][:, :, :], route(r0["top"][:, :]), ALU.subtract)\
                        .then_inc(s["r_shifted"], 1)
                    step(tt(r["first"][:, :, :], r["logit"][:, :, :], route(r0["top"][:, :]), ALU.is_equal))
                    step(tt(r["cand"][:, :, :], r["first"][:, :, :], per_expert(const("first_wins")[0:RT, :]), ALU.mult))
                    step(dve.tensor_reduce(r0["best"][:, :], r["cand"][:, :, :], AX_X, ALU.max))
                    need(dve, "hT", y)
                    tt(onehot[:, :, :], r["cand"][:, :, :], route(r0["best"][:, :]), ALU.is_equal)\
                        .then_inc(s["onehot_ready"], 1)
                if live(v_):
                    grow(64, 6)
                if live(y):
                    need(dve, "exps_ready", y + 1)
                    step(dve.tensor_reduce(r0["total"][:, :], r["exps"][:, :, :], AX_X, ALU.add))
                    need(dve, "pay_u", y * RM)
                    dve.reciprocal(r0["prob"][:, :], r0["total"][:, :]).then_inc(s["prob_ready"], 1)
                    need(dve, "onehot_ready", y + 1)
                    step(tt(r["based"][:, :, :], onehot[:, :, :], per_expert(const("slot_base")[0:RT, :]), ALU.mult))
                    step(dve.tensor_reduce(r0["base"][:, :], r["based"][:, :, :], AX_X, ALU.add))
                if live(u):
                    need(dve, "v_mm", u + 1)
                    need(dve, "av", u - 1)
                    tt(v[par][:, :, 0:P], bk[1][:, :].rearrange("p (m f) -> p m f", m=NT),
                       bv[:, :].rearrange("p (o f) -> p o f", o=1).to_broadcast([P, NT, P]), ALU.add)\
                        .then_inc(s["v_ready"], 1)
                if live(y):
                    need(dve, "hT", y + 1)
                    rk = bk[7][0:RT, 96:96 + (RM + 1) * E].rearrange("p (m e) -> p m e", e=E)
                    need(dve, "ranks_read", y)
                    step(tt(r["rank"][:, :, :], rk[:, 0:RM, :], per_expert(seen[:, :]), ALU.add))
                    tt(seen[:, :], rk[:, RM, :], seen[:, :], ALU.add).then_inc(s["ranks_read"], 1)
                    step(tt(r["ranked"][:, :, :], r["rank"][:, :, :], onehot[:, :, :], ALU.mult))
                    step(dve.tensor_reduce(r0["rank"][:, :], r["ranked"][:, :, :], AX_X, ALU.add))
                    step(ts(r0["over"][:, :], r0["rank"][:, :], float(CAP), NOWHERE, ALU.is_gt, ALU.mult))
                    step(stt(r0["slotf"][:, :], r0["rank"][:, :], -1.0, r0["base"][:, :], ALU.add, ALU.add))
                    if live(y, 2):
                        dma_slot(dve, "sent", y, par)
                    tt(slot[par][:, :], r0["slotf"][:, :], r0["over"][:, :], ALU.add).then_inc(s["slot_ready"], 1)
                    need(dve, "prob_ready", y + 1)
                    dve.tensor_copy(pay[par][:, :, 2 * P], r0["prob"][:, :])
                    step(dve.tensor_copy(pay[par][:, :, 2 * P + 1], r0["tok"][:, :]))
                    step(ts(r0["tok"][:, :], r0["tok"][:, :], float(W), None, ALU.add))
                if live(v_):
                    need(dve, "av", v_ + 1)
                    pd = near_ps[:, :, 0:TPB * (P + 1)].rearrange("p b (t f) -> p b t f", t=TPB)
                    ts(den[:, :, :], pd[:, :, :, P], ATTN_EPS, None, ALU.add).then_inc(s["den_ready"], 1)
                    need(dve, "den_ready", v_ + 1)
                    dve.reciprocal(rden[:, :, :], den[:, :, :]).then_inc(s["rden_ready"], 1)
                    need(dve, "rden_ready", v_ + 1)
                    need(dve, "mixed_T", v_)
                    for b in range(BU):
                        mx = tt(mixed[:, b * TPB:(b + 1) * TPB, :], pd[:, b, :, 0:P],
                                rden[:, b, :].rearrange("p (t o) -> p t o", o=1).to_broadcast([P, TPB, P]), ALU.mult)
                    mx.then_inc(s["mixed_ready"], 1)
                if live(y):
                    need(dve, "pay_h", y * 2 + 2)
                    need(dve, "pay_u", y * RM + RM)
                    if live(y, 2):
                        dma_slot(dve, "plain_out", y, par)
                    tt(plain[par][:, :, :], pay[par][:, :, 0:P], pay[par][:, :, P:2 * P], ALU.add)\
                        .then_inc(s["plain_ready"], 1)
                if live(v_):
                    need(dve, "mixed_T", v_ + 1)
                    need(dve, "h2", v_ + 1)
                    need(dve, "hT", v_ - 1)
                    tt(h3[vp][:, :], seg(h, v_), far_ps[:, 0, 0:W], ALU.add).then_inc(s["h3"], 1)

            units(dve, body, 2)

            def finish(t, par):
                e = 2 * t + par
                bias = bexp[:, bass.ds(e, 1), :].rearrange("p e f -> p (e f)")
                need(dve, "expert_y", e + 1)
                if not isinstance(t, int) or t > 0:
                    dve.wait_ge(s[f"done{par}"], t * (16 * EM))
                for m in range(EM):
                    f = stt(res[par][:, m, :], bias, rows[par][:, m, 2 * P:2 * P + 1],
                            pair[1][0:ET, m // 4, (m % 4) * P:(m % 4 + 1) * P], ALU.mult, ALU.add)
                f.then_inc(s["res_mm"], 1)
                dve.tensor_copy(where[par][:, :], rows[par][:, :, 2 * P + 1]).then_inc(s["where_ready"], 1)
                need(dve, "res_mm", e + 1)
                tt(res[par][:, :, :], res[par][:, :, :], rows[par][:, :, P:2 * P], ALU.add).then_inc(s["res_ready"], 1)

            finish(0, 0)
            finish(0, 1)
            with dve.Fori(1, E // 2) as t:
                finish(t, 0)
                finish(t, 1)


def kernel(**inputs):
    import numpy as np
    import concourse.bacc as _bacc
    from concourse import mybir as _mybir
    from concourse.bass_utils import run_bass_kernel_spmd as _run

    i = {k: np.asarray(v) for k, v in inputs.items()}

    def conv_w(w):
        return np.ascontiguousarray(w.T.reshape(-1, P, P).transpose(1, 0, 2))

    col = lambda a: a.reshape(-1, 1)
    x = i["x"]
    x2 = np.ascontiguousarray(np.concatenate([x[:, 0:XT], x[:, 1:S_IN]], axis=2).transpose(2, 0, 1))
    z = np.zeros((P, 1), np.float32)
    cols = [col(i["L0_tok_b0"]), col(i["L0_tok_b1"]), col(i["L0_tok_b2"]),
            col(np.concatenate([i["L0_attn_A_real"]] * 2)), col(np.concatenate([i["L0_attn_A_imag"]] * 2)),
            col(i["L0_attn_D_vec"]), col(i["L1_attn_bq"]), col(i["L1_attn_bk"]), col(i["L1_attn_ba"])]
    cols = np.concatenate(cols + [z] * (16 - len(cols)), axis=1)
    arrays = {
        "x2": x2, "wconv2": conv_w(i["L0_tok_W2"]), "wconv1": conv_w(i["L0_tok_W1"]), "wconv0": conv_w(i["L0_tok_W0"]),
        "cols": cols, "pos": np.ascontiguousarray(i["L0_tok_pos"][0, 0:L].T),
        "cst": constants(),
        "wg": i["L0_ffn_Wg"], "bg": np.tile(i["L0_ffn_bg"], (B, 1)), "be": i["L0_ffn_be"], "we": i["L0_ffn_We"],
        "bv": np.tile(i["L1_attn_bv"], (P, 1)),
        "wqkav": np.ascontiguousarray(np.stack([i[f"L1_attn_W{n}"].T for n in "qkav"], axis=1)),
        "wswitch": np.ascontiguousarray(i["L1_ffn_switch_w"].T), "bswitch": np.tile(i["L1_ffn_switch_b"], (RT, 1)),
        "wexp": np.ascontiguousarray(i["L1_ffn_expert_w"].transpose(2, 0, 1)),
        "bexp": np.tile(i["L1_ffn_expert_b"][None], (ET, 1, 1)),
        "ssm_in": np.ascontiguousarray(np.concatenate([i["L0_attn_B_mat"]] * 2).T),
        "ssm_out": np.ascontiguousarray(np.concatenate([i["L0_attn_C_mat"].T] * 2)),
    }
    nc = _bacc.Bacc("TRN2", target_bir_lowering=False, num_devices=1)
    args, sent = {}, {}
    for name, a in arrays.items():
        sent[f"in_{name}"] = a
        args[name] = nc.dram_tensor(f"in_{name}", a.shape, _mybir.dt.from_np(a.dtype), kind="ExternalInput").ap()
    slots = nc.dram_tensor("slots", (E * REGION, ROW), F32, kind="Internal").ap()
    out = nc.dram_tensor("out_0", (NTOK, P), F32, kind="ExternalOutput").ap()
    bass_audio_tower_kernel(nc, args, slots, out)
    r = _run(nc, [sent], core_ids=[0])
    return r.results[0]["out_0"].reshape(B, L, P)


def constants():
    import numpy as np
    p = np.arange(P)
    t = np.arange(32)[None, :]
    j = (p % 32)[:, None]
    eye = np.eye(P)
    parts = {
        "ident": eye, "center": eye - 1.0 / P, "mean": np.full((P, P), 1.0 / P), "ones": np.ones((P, P)),
        "upper": (p[:, None] <= p[None, :]), "diag32": j == t,
        "first_wins": np.tile(E - np.arange(E), (P, 1)), "slot_base": np.tile(np.arange(E) * REGION, (P, 1)), "expert_id": np.tile(np.arange(E), (P, 1)),
        "token": p[:, None] + np.arange(RM)[None, :] * RT,
    }
    for s in LEVELS:
        parts[f"level{s}"] = (j // (2 * s) == t // (2 * s)) & (j % (2 * s) < s) & (t % (2 * s) >= s)
    return np.concatenate([np.asarray(parts[n], np.float32) for n, _ in CONSTS], axis=1)
```

```python
from contextlib import ExitStack

import concourse.bass as bass
from concourse import mybir

ALU = mybir.AluOpType
ACT = mybir.ActivationFunctionType
AX_X = mybir.AxisListType.X
F32 = mybir.dt.float32
BF16 = mybir.dt.bfloat16
I32 = mybir.dt.int32

P = 128
B = 32
S_IN = 250
D_IN = 64
PATCH = 16
L = S_IN - PATCH + 1
BU = 2
W = BU * L
U = B // BU
NTOK = B * L
TAPS = PATCH // 2
XT = S_IN - 1
N_STATE = 64
E = 16
LN_EPS = 1e-5
ATTN_EPS = 1e-6
TILE = 128
TPB = 2
LP = TPB * TILE
NT = BU * TPB
CAP = int(1.2 * NTOK / E)
EM = CAP // P
REST = CAP - EM * P
HALF = P // 2
FILL = 6
HEAD = U * NT * P - NTOK
ROW = 2 * P + 2
NOWHERE = 1.0e6
DT = 0.01
DAMP_MIN = 0.0005
LN_EXP = "natural_log_exp_and_others"
SIGMOID = "sigmoid_and_others"
WB_IN = 16 * 9
PADS = 2 * 4 + 6
R_STEPS = 9
LV = 14

LEVELS = [1, 2, 4, 8, 16]
CONSTS = [("ident", P), ("center", P), ("mean", P), ("ones", P), ("upper", P), ("diag32", 32)] + \
    [(f"level{s}", 32) for s in LEVELS] + [("first_wins", NT * E), ("expert_id", E), ("slot_of", NT), ("token", NT)]
C_OFF = {}
C_W = 0
for _n, _w in CONSTS:
    C_OFF[_n] = (C_W, C_W + _w)
    C_W += _w


def bass_audio_tower_kernel(nc, ins, slots, out):
    ctx = ExitStack()
    with ctx:
        def sb(name, shape, dt=F32):
            return ctx.enter_context(nc.sbuf_tensor(name, shape, dt))

        def pb(name, n=1):
            return ctx.enter_context(nc.psum_tensor(name, [P, n, 512], F32))

        def sem(name):
            return ctx.enter_context(nc.semaphore(name))

        cst = sb("cst", [P, C_W])

        def const(name):
            a, b = C_OFF[name]
            return cst[:, a:b]

        h = sb("h", [P, U * NT * P])
        u2 = sb("u2", [P, NTOK])
        xin = [sb(f"xin{i}", [P, BU, XT]) for i in range(2)]
        wconv = sb("wconv", [P, TAPS, P])
        wconv1 = sb("wconv1", [P, TAPS // 2, P])
        wconv0 = sb("wconv0", [P, TAPS // 4, P])
        posb = sb("posb", [P, L])
        cols = sb("cols", [P, 16])
        ssm_in = sb("ssm_in", [P, P])
        ssm_out = sb("ssm_out", [P, P])
        tab = sb("tab", [P, 24])
        cosn = sb("cosn", [P, 256])
        sinn = sb("sinn", [P, 256])
        tmpn = sb("tmpn", [P, 256])
        tin = sb("tin", [P, L])
        tout = sb("tout", [P, L])
        decay = sb("decay", [P, BU, L])
        sq = sb("sq", [P, W])
        std = sb("std", [P, W])
        rstd = sb("rstd", [P, W])
        sq2 = sb("sq2", [P, W])
        std2 = sb("std2", [P, W])
        rstd2 = sb("rstd2", [P, W])
        u1 = sb("u1", [P, W])
        vin = sb("vin", [P, W])
        state = sb("state", [P, W])
        msum = sb("msum", [P, B])
        eps = sb("eps", [P, 1])

        wg = sb("wg", [P, E])
        gate_b = sb("gate_b", [B, E])
        be0 = sb("be0", [E, P])
        gs = sb("gs", [B, 8 * E])
        gT = sb("gT", [E, B])
        pick_f = sb("pick_f", [B, 1])
        pick = sb("pick", [1, B], I32)
        gate = sb("gate", [P, B])
        gbias = sb("gbias", [P, B])
        wsel = [sb(f"wsel{i}", [P, BU, P]) for i in range(2)]
        ffn = sb("ffn", [P, W])
        wqkav = sb("wqkav", [P, 4, P])
        bv = sb("bv", [P, P])
        u3 = [sb(f"u3{i}", [P, BU, LP]) for i in range(2)]
        q = [sb(f"q{i}", [P, BU, LP]) for i in range(2)]
        k = [sb(f"k{i}", [P, BU, LP]) for i in range(2)]
        a = [sb(f"a{i}", [P, BU, LP]) for i in range(2)]
        v = [sb(f"v{i}", [P, NT, P + 1]) for i in range(2)]
        qs = [sb(f"qs{i}", [P, BU * LP]) for i in range(2)]
        prod = {n: sb(f"prod{n}", [P, BU * LP // n]) for n in (2, 4, 8, 16, 32, 64)}
        near = sb("near", [P, NT, 32])
        attn = sb("attn", [P, BU, 3, P])
        den = sb("den", [P, BU, TPB])
        rden = sb("rden", [P, BU, TPB])
        u4 = sb("u4", [P, NT * P])
        h2f = sb("h2f", [P, W])
        u3t = sb("u3t", [P, NT, P])
        u4t = sb("u4t", [P, NT, P])
        ln = [{n: sb(f"ln{i}_{n}", [P, NT] + w)
               for n, w in (("stats", [6]), ("agg", [2]), ("log", []), ("rstd", []), ("shift", []))}
              for i in (3, 4)]
        wswitch = sb("wswitch", [P, E])
        bswitch = sb("bswitch", [P, E])
        upper_bf = sb("upper_bf", [P, P], BF16)
        ones_bf = sb("ones_bf", [P, P], BF16)
        r1 = {n: sb(f"r_{n}", [P, NT, E]) for n in "logit shifted exps first rank ranked".split()}
        cand = sb("cand", [P, NT, E + 1])
        turn_dve = sb("turn_dve", [1, 2])
        onehot = sb("onehot", [P, NT, E], BF16)
        r0 = {n: sb(f"r0_{n}", [P, NT]) for n in "top best total prob rank base over slotf tok".split()}
        slot = [sb(f"slot{i}", [P, NT], I32) for i in range(2)]
        seen = sb("seen", [P, E])
        pay = [sb(f"pay{i}", [P, NT, ROW]) for i in range(2)]
        plain = [sb(f"plain{i}", [P, NT, P]) for i in range(2)]
        turn = sb("turn", [1, 2])
        empty = sb("empty", [CAP // FILL, FILL, ROW])
        wexp = sb("wexp", [P, E, P])
        bexp = sb("bexp", [P, E, P])
        rows = [sb(f"rows{i}", [P, EM, ROW]) for i in range(2)]
        ut = sb("ut", [P, EM, P])
        res = [sb(f"res{i}", [P, EM, P]) for i in range(2)]
        where = [sb(f"where{i}", [P, EM], I32) for i in range(2)]
        rest = sb("rest", [P, ROW])
        rest_ut = sb("rest_ut", [P, 2, P])
        rest_res = sb("rest_res", [P, P])
        rest_where = sb("rest_where", [P, 1], I32)

        pair = [pb(f"pair{i}", 2) for i in range(4)]
        psH0, psC, psV, psB, psY, psC2, psV2, psH1 = [p[:, i, :] for p in pair for i in range(2)]
        psH = [psH0, psH1]
        bk = [p[:, i, :] for p in pair for i in range(2)]
        near_ps, far_ps = pair[1], pair[2]

        names = """
            cst_in weights_in cols_in ssm_in_dma wb_in conv_w x0 x1
            dve_setup tables eps_ready empty_ready turn_ready prefilled route_bf pads_ready
            conv_done h0 cen1 sq1 var1 std1 rstd1 u1_ready bu vin_ready scan_done state_ready y1 dterm h1
            cen2 sq2_ready var2 std2_ready rstd2_ready u2_ready msum_ready
            gate_pe gate_dve gate_act pick_ready wsel0 wsel1
            ffn_y ffn_done h2 h2T h2_ready stats3 agg3 log3 rstd3 u3_normed u3T u3_ready
            q_mm k_mm a_mm v_mm q_ready k_ready a_ready v_ready
            qs_ready lv1 lv2 lv4 lv8 lv16 lv32 lv64 lv128 diag_ready grown near_placed far_placed cross_placed
            av den_ready rden_ready h3
            stats4 agg4 log4 rstd4 shift4 u4_normed u4T u4_ready logits
            r_dve r_shifted exps_ready onehot_ready prob_ready ranks ranks_read ranked marked slot_parts
            pay_u slot_ready plain_ready plain_out0 plain_out1 sent0 sent1
            rows0 rows1 rowsT ut_ready expert_y res_mm res_ready where_ready done0 done1
            rest_in restT rest_ut_ready rest_y rest_mm rest_ready rest_where_ready rest_done""".split()
        s = {n: sem(n) for n in names}

        def units(eng, body, depth):
            peel = depth + depth % 2 + 2
            for u in range(peel):
                body(u, u % 2)
            with eng.Fori(peel // 2, U // 2) as k:
                body(2 * k, 0)
                body(2 * k + 1, 1)
            for u in range(U, U + depth):
                body(u, u % 2)

        def live(u, k=0):
            return not isinstance(u, int) or 0 <= u - k < U

        def need(eng, name, value):
            if not isinstance(value, int) or value > 0:
                eng.wait_ge(s[name], value)

        def dma_slot(eng, name, u, par):
            each = 16 * (NT if name == "sent" else 2)
            eng.wait_ge(s[f"{name}{par}"], u // 2 * each if isinstance(u, int) else (u - par) * (each // 2))

        def seg(t, u):
            return t[:, bass.ds(u * W + (HEAD if t is h else 0), W)]

        def by_token(u):
            return h[:, bass.ds(u * (NT * P), NT * P)].rearrange("p (m f) -> p m f", m=NT)

        def two(ap):
            return ap.rearrange("p (b t) -> p b t", b=BU)

        def near_at(n, b):
            c = TPB * 32 if n == 1 else 0
            return near_ps[:, b, c:c + TPB * 32]

        block = ctx.enter_context(nc.Block())

        @block.sync
        def _(sp):
            sp.dma_start(wconv[:, :, :], ins["wconv2"]).then_inc(s["weights_in"], 16)
            sp.dma_start(wconv1[:, :, :], ins["wconv1"]).then_inc(s["weights_in"], 16)
            sp.dma_start(wconv0[:, :, :], ins["wconv0"]).then_inc(s["weights_in"], 16)

            def load_x(k, par):
                u = 2 * k + par
                need(sp, "conv_done", u - 1)
                sp.dma_start(xin[par][:, :, :], ins["x2"][:, bass.ds(u * BU, BU), :]).then_inc(s[f"x{par}"], 16)

            sp.dma_start(cst[:, :], ins["cst"]).then_inc(s["cst_in"], 16)
            sp.dma_start(ssm_in[:, :], ins["ssm_in"]).then_inc(s["ssm_in_dma"], 16)
            sp.dma_start(ssm_out[:, :], ins["ssm_out"]).then_inc(s["ssm_in_dma"], 16)
            load_x(0, 1)
            for dst, name in ((wg, "wg"), (gate_b, "bg"), (be0, "be"), (bv, "bv"), (wswitch, "wswitch"),
                              (bswitch, "bswitch")):
                sp.dma_start(dst[:, :], ins[name]).then_inc(s["wb_in"], 16)
            sp.dma_start(wqkav[:, :, :], ins["wqkav"]).then_inc(s["wb_in"], 16)
            load_x(1, 0)
            load_x(1, 1)
            sp.dma_start(wexp[:, :, :], ins["wexp"]).then_inc(s["wb_in"], 16)
            sp.dma_start(bexp[:, :, :], ins["bexp"]).then_inc(s["wb_in"], 16)
            with sp.Fori(2, U // 2) as k:
                load_x(k, 0)
                load_x(k, 1)
            def load_expert(k, par):
                u = 2 * k + par
                need(sp, "ffn_y", u - 1)
                for b in range(BU):
                    e = sp.value_load(pick[0:1, bass.ds(u * BU + b, 1)], min_val=0, max_val=E - 1)
                    sp.dma_start(wsel[par][:, b, :], ins["we"][bass.ds(e, 1), :, :].rearrange("e d o -> (e d) o"))\
                      .then_inc(s[f"wsel{par}"], 16)

            def store_plain(k, par):
                u = 2 * k + par
                need(sp, "plain_ready", u + 1)
                dst = out[bass.ds(u * W, W), :].rearrange("(b t) f -> t b f", b=BU)
                src = plain[par][:, :, :].rearrange("p (b t) f -> p b t f", b=BU)
                sp.dma_start(dst[0:TILE], src[:, :, 0, :]).then_inc(s[f"plain_out{par}"], 16)
                sp.dma_start(dst[TILE:L], src[0:L - TILE, :, 1, :]).then_inc(s[f"plain_out{par}"], 16)

            sp.wait_ge(s["pick_ready"], 1)
            load_expert(0, 0)
            load_expert(0, 1)
            for t in range(1, 3):
                load_expert(t, 0)
                load_expert(t, 1)
            store_plain(0, 0)
            with sp.Fori(3, U // 2) as t:
                load_expert(t, 0)
                store_plain(t - 3, 1)
                load_expert(t, 1)
                store_plain(t - 2, 0)
            store_plain(U // 2 - 3, 1)
            for t in range(U // 2 - 2, U // 2):
                store_plain(t, 0)
                store_plain(t, 1)

            for par in range(2):
                sp.wait_ge(s[f"sent{par}"], 16 * NT * U // 2)
                sp.wait_ge(s[f"plain_out{par}"], 32 * U // 2)

            def load_rows(t, par):
                e = 2 * t + par
                need(sp, "res_ready", e - 1)
                need(sp, "where_ready", e - 1)
                sp.dma_start(rows[par][:, :, :],
                             slots[bass.ds(e * CAP, EM * P), :].rearrange("(p m) c -> p m c", m=EM))\
                  .then_inc(s[f"rows{par}"], 16)

            def load_rest(t):
                need(sp, "rest_ready", t)
                need(sp, "rest_where_ready", t)
                for half in range(2):
                    sp.dma_start(rest[half * HALF:half * HALF + REST, :],
                                 slots[bass.ds((2 * t + half) * CAP + EM * P, REST), :]).then_inc(s["rest_in"], 16)

            sp.wait_ge(s["pads_ready"], PADS)
            load_rows(0, 0)
            load_rows(0, 1)
            load_rest(0)
            with sp.Fori(1, E // 2) as t:
                load_rows(t, 0)
                load_rows(t, 1)
                load_rest(t)

        @block.gpsimd
        def _(pool):
            pool.memset(empty[:, :, :], 0.0).then_inc(s["empty_ready"], 1)
            pool.wait_ge(s["empty_ready"], 1)
            pool.memset(empty[:, :, ROW - 1:ROW], NOWHERE).then_inc(s["empty_ready"], 1)
            for t in q + k:
                pool.memset(t[:, :, L:LP], 0.0).then_inc(s["pads_ready"], 1)
            for t in a:
                pool.memset(t[:, :, L:LP], 1.0).then_inc(s["pads_ready"], 1)
            for t in v:
                pool.memset(t[:, :, P:P + 1], 1.0).then_inc(s["pads_ready"], 1)
            pool.memset(h[:, 0:HEAD], 0.0).then_inc(s["pads_ready"], 1)
            pool.memset(cand[:, :, E:E + 1], 0.5).then_inc(s["pads_ready"], 1)
            pool.memset(attn[:, :, :, :], 0.0).then_inc(s["pads_ready"], 1)
            pool.memset(rest[:, :], NOWHERE).then_inc(s["pads_ready"], 1)
            pool.memset(rest_res[:, :], 0.0).then_inc(s["pads_ready"], 1)
            pool.memset(rest_ut[:, :, :], 0.0).then_inc(s["pads_ready"], 1)
            pool.wait_ge(s["pads_ready"], PADS)
            pool.memset(turn[:, :], 0.0).then_inc(s["turn_ready"], 1)
            pool.wait_ge(s["turn_ready"], 1)

            def gate_dmas(n):
                need(pool, "turn_ready", n + 1)
                pool.tensor_tensor(turn[:, 0:1], turn[:, 1:2], turn[:, 1:2], ALU.add).then_inc(s["turn_ready"], 1)

            def body(u, par):
                y = u - 4
                yp = par
                if live(y):
                    need(pool, "pay_u", y * NT + NT)
                    if live(y, 2):
                        dma_slot(pool, "plain_out", y, yp)
                    pool.tensor_tensor(plain[yp][:, :, :], pay[yp][:, :, 0:P], pay[yp][:, :, P:2 * P], ALU.add)\
                        .then_inc(s["plain_ready"], 1)
                    need(pool, "slot_ready", y + 1)
                    need(pool, "plain_ready", y + 1)
                    gate_dmas(y)
                    for m in range(NT):
                        pool.indirect_dma_start(
                            out=slots, out_offset=bass.IndirectOffsetOnAxis(ap=slot[yp][:, m:m + 1], axis=0),
                            in_=pay[yp][:, m, :], in_offset=None, bounds_check=E * CAP - 1, oob_is_err=False)\
                            .then_inc(s[f"sent{yp}"], 16)

            pool.wait_ge(s["prefilled"], 16 * E)
            units(pool, body, 4)

            def scatter(t, par):
                e = 2 * t + par
                need(pool, "res_ready", e + 1)
                need(pool, "where_ready", e + 1)
                gate_dmas(U + 3 * t + par)
                for m in range(EM):
                    pool.indirect_dma_start(
                        out=out, out_offset=bass.IndirectOffsetOnAxis(ap=where[par][:, m:m + 1], axis=0),
                        in_=res[par][:, m, :], in_offset=None, bounds_check=NTOK - 1, oob_is_err=False)\
                        .then_inc(s[f"done{par}"], 16)

            def scatter_rest(t):
                need(pool, "rest_ready", t + 1)
                need(pool, "rest_where_ready", t + 1)
                gate_dmas(U + 3 * t + 2)
                pool.indirect_dma_start(
                    out=out, out_offset=bass.IndirectOffsetOnAxis(ap=rest_where[:, 0:1], axis=0),
                    in_=rest_res[:, :], in_offset=None, bounds_check=NTOK - 1, oob_is_err=False)\
                    .then_inc(s["rest_done"], 16)

            for par in range(2):
                pool.wait_ge(s[f"plain_out{par}"], 32 * U // 2)
            with pool.Fori(0, E // 2) as t:
                scatter(t, 0)
                scatter(t, 1)
                scatter_rest(t)
            for par in range(2):
                pool.wait_ge(s[f"done{par}"], 16 * EM * E // 2)
            pool.wait_ge(s["rest_done"], 16 * E // 2)

        @block.tensor
        def _(pe):
            pe.wait_ge(s["conv_w"], 1)

            def x_wait(u, par):
                if isinstance(u, int):
                    pe.wait_ge(s[f"x{par}"], 16 * (u // 2 + 1))
                else:
                    pe.wait_ge(s[f"x{par}"], (u - par) * 8 + 16)

            def conv(u, par, a, b):
                for j in range(a, b):
                    mm = pe.matmul(psH[par][:, 0:W], wconv[:, j, :], xin[par][:, :, 2 * j:2 * j + L],
                                   start=(j == 0), stop=(j == TAPS - 1))
                if b == TAPS:
                    mm.then_inc(s["conv_done"], 1)

            def body(u, par):
                v, y = u - 1, u - 2
                if live(u):
                    x_wait(u, par)
                    need(pe, "h0", u - 1)
                    conv(u, par, 0, 2)
                if live(v):
                    need(pe, "h0", v + 1)
                    need(pe, "u1_ready", v)
                    pe.matmul(psC[:, 0:W], const("center"), seg(h, v), start=True, stop=True).then_inc(s["cen1"], 1)
                if live(y):
                    need(pe, "state_ready", y + 1)
                    need(pe, "h1", y)
                    pe.matmul(psY[:, 0:W], ssm_out[:, :], state[:, :], start=True, stop=True).then_inc(s["y1"], 1)
                if live(u):
                    conv(u, par, 2, 4)
                if live(y):
                    need(pe, "h1", y + 1)
                    need(pe, "u2_ready", y)
                    pe.matmul(psC2[:, 0:W], const("center"), seg(h, y), start=True, stop=True).then_inc(s["cen2"], 1)
                if live(v):
                    need(pe, "sq1", v + 1)
                    need(pe, "std1", v)
                    pe.matmul(psV[:, 0:W], const("mean"), sq[:, :], start=True, stop=True).then_inc(s["var1"], 1)
                if live(u):
                    conv(u, par, 4, 6)
                if live(y):
                    need(pe, "sq2_ready", y + 1)
                    need(pe, "std2_ready", y)
                    pe.matmul(psV2[:, 0:W], const("mean"), sq2[:, :], start=True, stop=True).then_inc(s["var2"], 1)
                if live(u):
                    conv(u, par, 6, 7)
                if live(v):
                    need(pe, "u1_ready", v + 1)
                    need(pe, "vin_ready", v)
                    pe.matmul(psB[:, 0:W], ssm_in[:, :], u1[:, :], start=True, stop=True).then_inc(s["bu"], 1)
                if live(u):
                    conv(u, par, 7, 8)

            pe.wait_ge(s["cst_in"], 16)
            pe.wait_ge(s["ssm_in_dma"], 32)
            units(pe, body, 2)

            gps = bk[0]
            pe.wait_ge(s["wb_in"], WB_IN)
            pe.wait_ge(s["msum_ready"], U)
            pe.wait_ge(s["h0"], U)
            pe.wait_ge(s["vin_ready"], U)
            pe.wait_ge(s["h1"], U)
            pe.matmul(gps[0:B, 0:E], msum[:, :], wg[:, :], start=True, stop=True).then_inc(s["gate_pe"], 1)
            pe.wait_ge(s["gate_dve"], 2)
            pe.matmul(bk[1][0:E, 0:B], gs[:, 3 * E:4 * E], const("ident")[0:B, 0:B], start=True, stop=True)
            pe.matmul(bk[2][0:1, 0:B], pick_f[:, :], const("ident")[0:B, 0:B], start=True, stop=True)\
              .then_inc(s["gate_pe"], 1)
            pe.wait_ge(s["gate_dve"], 3)
            pe.matmul(bk[3][:, 0:B], const("ones")[0:E, :], gT[:, :], start=True, stop=True)
            pe.matmul(bk[4][:, 0:B], be0[:, :], gT[:, :], start=True, stop=True).then_inc(s["gate_pe"], 1)
            pe.wait_ge(s["gate_dve"], 4)
            pe.wait_ge(s["pads_ready"], PADS)
            pe.wait_ge(s["route_bf"], 2)

            def near_level(n, b, kk, qq):
                for m in range(TPB):
                    for g in range(4):
                        at = b * LP + m * TILE + 32 * g
                        mm = pe.matmul(near_at(n, b)[32 * g:32 * g + 32, m * 32:m * 32 + 32],
                                       kk[:, at:at + 32], qq[:, at:at + 32], start=True, stop=True)
                return mm

            def far_level(b, kk, qq, size):
                for m in range(b * TPB, b * TPB + TPB):
                    for at in range(0, TILE, 2 * size):
                        c = m * TILE + at
                        mm = pe.matmul(far_ps[at:at + size, 0, c + size:c + 2 * size], kk[:, c:c + size],
                                       qq[:, c + size:c + 2 * size], start=True, stop=True)
                return mm

            def turned(dst, src, m):
                b, second = m // TPB, m % TPB
                n = L - TILE if second else TILE
                c = b * L + second * TILE
                return pe.transpose(dst[0:n, m * P:(m + 1) * P], src[:, c:c + n], const("ident"))

            def body(u, par):
                w, v_, y = u - 1, u - 2, u - 3
                wp, vp, yp = 1 - par, par, 1 - par
                kf = k[vp][:, :, :].rearrange("p b t -> p (b t)")
                qf = q[vp][:, :, :].rearrange("p b t -> p (b t)")

                def level(n, size):
                    if not live(v_):
                        return
                    for b in range(BU):
                        need(pe, "grown", v_ * LV + 2 * (n - 1) + b + 1)
                        if size < 32:
                            near_level(n + 1, b, kf, qs[vp]).then_inc(s[f"lv{size}"], 1)
                        else:
                            far_level(b, kf, qs[vp], size).then_inc(s[f"lv{size}"], 1)

                def projection(i, name):
                    pe.matmul(two(bk[i % 2][:, 0:W]), wqkav[:, i, :], u3[wp][:, :, 0:L], start=True, stop=True)\
                      .then_inc(s[name], 1)

                if live(v_):
                    need(pe, "qs_ready", v_ + 1)
                    need(pe, "k_ready", v_ + 1)
                    need(pe, "q_ready", v_ + 1)
                    for b in range(BU):
                        near_level(0, b, kf, qf)
                        near_level(1, b, kf, qs[vp]).then_inc(s["lv1"], 1)
                if live(y):
                    need(pe, "near_placed", y * 4 + 4)
                    need(pe, "far_placed", y * 3 + 3)
                    need(pe, "cross_placed", y + 1)
                    need(pe, "v_ready", y + 1)
                    for b in range(BU):
                        pe.matmul(far_ps[:, b, 0:P + 1], attn[:, b, 0, :], v[yp][:, b * TPB, :], start=True, stop=True)
                        pe.matmul(far_ps[:, b, P + 1:2 * P + 2], attn[:, b, 1, :], v[yp][:, b * TPB, :],
                                  start=True, stop=False)
                        mm = pe.matmul(far_ps[:, b, P + 1:2 * P + 2], attn[:, b, 2, :], v[yp][:, b * TPB + 1, :],
                                       start=False, stop=True)
                    mm.then_inc(s["av"], 1)
                level(1, 2)
                if live(u):
                    if isinstance(u, int):
                        pe.wait_ge(s[f"wsel{par}"], 32 * (u // 2 + 1))
                    else:
                        pe.wait_ge(s[f"wsel{par}"], (u - par) * 16 + 32)
                    need(pe, "a_ready", w)
                    for b in range(BU):
                        mm = pe.matmul(bk[0][:, b * L:(b + 1) * L], wsel[par][:, b, :],
                                       u2[:, bass.ds(u * W + b * L, L)], start=True, stop=True)
                    mm.then_inc(s["ffn_y"], 1)
                if live(w):
                    if live(u):
                        need(pe, "ffn_done", u + 1)
                    else:
                        need(pe, "a_ready", w)
                    need(pe, "u3_ready", w + 1)
                    projection(0, "q_mm")
                level(2, 4)
                if live(w):
                    need(pe, "q_ready", w + 1)
                    projection(2, "a_mm")
                if live(u):
                    need(pe, "h2", u + 1)
                    need(pe, "u3_ready", u)
                    for m in range(NT):
                        mm = turned(bk[6], h2f, m)
                    mm.then_inc(s["h2T"], 1)
                level(3, 8)
                if live(w):
                    need(pe, "v_ready", w)
                    projection(1, "k_mm")
                if live(y):
                    need(pe, "u4_normed", y + 1)
                    if live(u):
                        need(pe, "h2_ready", u + 1)
                    for m in range(NT):
                        mm = pe.transpose(bk[6][:, m * P:(m + 1) * P], u4t[:, m, :], const("ident"))
                    mm.then_inc(s["u4T"], 1)
                level(4, 16)
                if live(y):
                    need(pe, "u4_ready", y + 1)
                    need(pe, "ranks_read", y)
                    for m in range(NT):
                        mm = pe.matmul(bk[7][:, m * E:(m + 1) * E], u4[:, m * P:(m + 1) * P], wswitch[:, :],
                                       start=True, stop=True)
                    mm.then_inc(s["logits"], 1)
                if live(v_):
                    need(pe, "far_placed", v_ * 3)
                    need(pe, "h3", v_)
                level(5, 32)
                if live(w):
                    need(pe, "k_ready", w + 1)
                    for m in range(NT):
                        mm = pe.matmul(bk[1][:, m * P:(m + 1) * P],
                                       u3[wp][:, m // TPB, (m % TPB) * TILE:(m % TPB + 1) * TILE], wqkav[:, 3, :],
                                       start=True, stop=True)
                    mm.then_inc(s["v_mm"], 1)
                level(6, 64)
                if live(v_):
                    for b in range(BU):
                        need(pe, "grown", v_ * LV + 12 + b + 1)
                        mm = pe.matmul(far_ps[:, 1, b * P:(b + 1) * P], kf[:, b * LP:b * LP + TILE],
                                       qs[vp][:, b * LP + TILE:(b + 1) * LP], start=True, stop=True)
                    mm.then_inc(s["lv128"], 1)
                if live(u):
                    need(pe, "u3_normed", u + 1)
                    if live(y):
                        need(pe, "u4_ready", y + 1)
                    for m in range(NT):
                        mm = pe.transpose(bk[6][:, m * P:(m + 1) * P], u3t[:, m, :], const("ident"))
                    mm.then_inc(s["u3T"], 1)
                if live(y):
                    need(pe, "onehot_ready", y + 1)
                    oh = onehot[:, :, :].rearrange("p m e -> p (m e)")
                    pe.matmul(bk[7][:, 96:96 + NT * E], upper_bf[:, :], oh[:, 0:NT * E], start=True, stop=False,
                              skip_group_check=True)
                    for d in range(1, NT + 1):
                        mm = pe.matmul(bk[7][:, 96 + d * E:96 + (NT + 1) * E], ones_bf[:, :], oh[:, 0:(NT + 1 - d) * E],
                                       start=False, stop=(d == NT), skip_group_check=True)
                    mm.then_inc(s["ranks"], 1)

            units(pe, body, 4)

            pe.wait_ge(s["h3"], U)

            def expert(t, par):
                e = 2 * t + par
                if isinstance(t, int):
                    pe.wait_ge(s[f"rows{par}"], 16 * (t + 1))
                else:
                    pe.wait_ge(s[f"rows{par}"], t * 16 + 16)
                need(pe, "ut_ready", e)
                for m in range(EM):
                    mm = pe.transpose(bk[0][:, m * P:(m + 1) * P], rows[par][:, m, 0:P], const("ident"))
                mm.then_inc(s["rowsT"], 1)
                need(pe, "ut_ready", e + 1)
                need(pe, "res_mm", e)
                for m in range(EM):
                    mm = pe.matmul(bk[2][:, m * P:(m + 1) * P], ut[:, m, :], weights(e), start=True, stop=True)
                mm.then_inc(s["expert_y"], 1)

            def weights(e):
                return wexp[:, bass.ds(e, 1), :].rearrange("p e f -> p (e f)")

            def expert_rest(t):
                pe.wait_ge(s["rest_in"], t * 32 + 32)
                need(pe, "rest_ut_ready", t)
                pe.transpose(bk[1][:, 0:P], rest[:, 0:P], const("ident")).then_inc(s["restT"], 1)
                need(pe, "rest_ut_ready", t + 1)
                need(pe, "rest_mm", t)
                for half in range(2):
                    mm = pe.matmul(bk[3][:, 0:P], rest_ut[:, half, :], weights(2 * t + half),
                                   start=(half == 0), stop=(half == 1))
                mm.then_inc(s["rest_y"], 1)

            expert(0, 0)
            expert(0, 1)
            expert_rest(0)
            with pe.Fori(1, E // 2) as t:
                expert(t, 0)
                expert(t, 1)
                expert_rest(t)

        @block.scalar
        def _(act):
            def body(u, par):
                v, y = u - 1, u - 2
                if live(v):
                    need(act, "cen1", v + 1)
                    need(act, "var1", v)
                    act.activation(sq[:, :], psC[:, 0:W], ACT.Square).then_inc(s["sq1"], 1)
                if live(y):
                    need(act, "cen2", y + 1)
                    need(act, "var2", y)
                    act.activation(sq2[:, :], psC2[:, 0:W], ACT.Square).then_inc(s["sq2_ready"], 1)
                if live(v):
                    need(act, "var1", v + 1)
                    need(act, "rstd1", v)
                    act.activation(std[:, :], psV[:, 0:W], ACT.Ln, bias=eps[:, :]).then_inc(s["std1"], 1)
                    need(act, "std1", v + 1)
                    need(act, "u1_ready", v)
                    act.activation(rstd[:, :], std[:, :], ACT.Exp, scale=-0.5).then_inc(s["rstd1"], 1)
                if live(y):
                    need(act, "var2", y + 1)
                    need(act, "rstd2_ready", y)
                    act.activation(std2[:, :], psV2[:, 0:W], ACT.Ln, bias=eps[:, :]).then_inc(s["std2_ready"], 1)
                    need(act, "std2_ready", y + 1)
                    need(act, "u2_ready", y)
                    act.activation(rstd2[:, :], std2[:, :], ACT.Exp, scale=-0.5).then_inc(s["rstd2_ready"], 1)

            act.preload_act_table_set("sqrt_and_others")
            act.dma_start(xin[0][:, :, :], ins["x2"][:, 0:BU, :]).then_inc(s["x0"], 16)
            act.dma_start(cols[:, :], ins["cols"]).then_inc(s["cols_in"], 16)
            act.dma_start(posb[:, :], ins["pos"]).then_inc(s["cols_in"], 16)
            act.wait_ge(s["eps_ready"], 1)
            act.wait_ge(s["tables"], 1)
            act.activation(tab[:, 12:13], tab[:, 11:12], ACT.Sqrt).then_inc(s["tables"], 1)
            act.wait_ge(s["conv_done"], 1)
            act.wait_ge(s["empty_ready"], 2)
            for e in range(E):
                act.dma_start(slots[e * CAP:(e + 1) * CAP, :].rearrange("(p m) c -> p m c", m=FILL),
                              empty[:, :, :])\
                   .then_inc(s["prefilled"], 16)
            act.preload_act_table_set(LN_EXP)
            units(act, body, 2)

            act.wait_ge(s["gate_dve"], 1)
            act.activation(gs[:, 2 * E:3 * E], gs[:, E:2 * E], ACT.Exp).then_inc(s["gate_act"], 1)
            act.wait_ge(s["gate_dve"], 4)
            act.wait_ge(s["pads_ready"], PADS)

            def rstd_of(n, stage, t):
                need(act, f"agg{stage}", n + 1)
                act.activation(t["log"][:, :], t["agg"][:, :, 1], ACT.Ln, bias=eps[:, :]).then_inc(s[f"log{stage}"], 1)
                need(act, f"log{stage}", n + 1)
                act.activation(t["rstd"][:, :], t["log"][:, :], ACT.Exp, scale=-0.5).then_inc(s[f"rstd{stage}"], 1)

            def body(u, par):
                w, v_, y = u - 1, u - 2, u - 3
                wp, yp = 1 - par, 1 - par
                if live(u):
                    need(act, "ffn_y", u + 1)
                    need(act, "h2", u)
                    for b in range(BU):
                        at = bass.ds(u * BU + b, 1)
                        f = act.activation(ffn[:, b * L:(b + 1) * L], bk[0][:, b * L:(b + 1) * L], ACT.Identity,
                                           bias=gbias[:, at], scale=gate[:, at])
                    f.then_inc(s["ffn_done"], 1)
                if live(w):
                    need(act, "q_mm", w + 1)
                    act.activation(q[wp][:, :, 0:L], two(bk[0][:, 0:W]), ACT.Relu, bias=cols[:, 6:7])\
                       .then_inc(s["q_ready"], 1)
                if live(y):
                    rstd_of(y, 4, ln[1])
                if live(u):
                    need(act, "h2T", u + 1)
                    ht = by_token(u).rearrange("p (b t) f -> p b t f", b=BU)
                    hp = bk[6].rearrange("p (b t f) -> p b t f", b=BU, t=TPB)
                    act.copy(ht[:, :, 0, :], hp[:, :, 0, :])
                    act.copy(ht[0:L - TILE, :, 1, :], hp[0:L - TILE, :, 1, :]).then_inc(s["h2_ready"], 1)
                if live(y):
                    need(act, "shift4", y + 1)
                    need(act, "pay_u", y * NT)
                    for m in range(NT):
                        nm = act.activation(u4t[:, m, :], pay[yp][:, m, P:2 * P], ACT.Identity,
                                            scale=ln[1]["rstd"][:, m:m + 1], bias=ln[1]["shift"][:, m:m + 1])
                    nm.then_inc(s["u4_normed"], 1)
                if live(w):
                    need(act, "k_mm", w + 1)
                    act.activation(k[wp][:, :, 0:L], two(bk[1][:, 0:W]), ACT.Relu, bias=cols[:, 7:8])\
                       .then_inc(s["k_ready"], 1)
                if live(y):
                    need(act, "u4T", y + 1)
                    act.copy(u4[:, :], bk[6]).then_inc(s["u4_ready"], 1)
                if live(u):
                    rstd_of(u, 3, ln[0])
                if live(v_):
                    need(act, "av", v_)
                    need(act, "grown", v_ * LV + 10)
                    for g in range(4):
                        act.copy(attn[32 * g:32 * g + 32, :, 0:3:2, 32 * g:32 * g + 32],
                                 near[32 * g:32 * g + 32, :, :].rearrange("p (b t) c -> p b t c", b=BU))\
                           .then_inc(s["near_placed"], 1)
                act.preload_act_table_set(SIGMOID)
                if live(w):
                    need(act, "a_mm", w + 1)
                    act.activation(a[wp][:, :, 0:L], two(bk[0][:, 0:W]), ACT.Sigmoid, bias=cols[:, 8:9])\
                       .then_inc(s["a_ready"], 1)
                act.preload_act_table_set(LN_EXP)
                if live(y):
                    need(act, "r_shifted", y + 1)
                    act.activation(r1["exps"][:, :, :], r1["shifted"][:, :, :], ACT.Exp).then_inc(s["exps_ready"], 1)
                if live(v_):
                    need(act, "lv64", v_ * 2 + 2)
                    for lo, n in ((0, 32), (64, 32), (0, 64)):
                        act.copy(attn[lo:lo + n, :, 0:3:2, lo + n:lo + 2 * n],
                                 far_ps[lo:lo + n, 0, :].rearrange("p (b t c) -> p b t c", b=BU, t=TPB)
                                 [:, :, :, lo + n:lo + 2 * n]).then_inc(s["far_placed"], 1)
                    need(act, "lv128", v_ + 1)
                    act.copy(attn[:, :, 1, :], far_ps[:, 1, 0:BU * P].rearrange("p (b c) -> p b c", b=BU))\
                       .then_inc(s["cross_placed"], 1)
                if live(u):
                    need(act, "u3T", u + 1)
                    act.copy(u3[par][:, :, :].rearrange("p b t -> p (b t)"), bk[6]).then_inc(s["u3_ready"], 1)
                if live(y):
                    need(act, "prob_ready", y + 1)
                    for m in range(NT):
                        act.activation(pay[yp][:, m, 0:P], u4t[:, m, :], ACT.Copy, scale=r0["prob"][:, m:m + 1])\
                           .then_inc(s["pay_u"], 1)

            units(act, body, 4)

            def turn_rows(t, par):
                e = 2 * t + par
                need(act, "rowsT", e + 1)
                need(act, "expert_y", e)
                act.copy(ut[:, :, :].rearrange("p m r -> p (m r)"), bk[0]).then_inc(s["ut_ready"], 1)

            def turn_rest(t):
                need(act, "restT", t + 1)
                need(act, "rest_y", t)
                act.copy(rest_ut[:, 0, 0:HALF], bk[1][:, 0:HALF])
                act.copy(rest_ut[:, 1, HALF:P], bk[1][:, HALF:P]).then_inc(s["rest_ut_ready"], 1)

            turn_rows(0, 0)
            turn_rows(0, 1)
            turn_rest(0)
            with act.Fori(1, E // 2) as t:
                turn_rows(t, 0)
                turn_rows(t, 1)
                turn_rest(t)

        @block.vector
        def _(dve):
            def over_batches(ap):
                return ap.rearrange("p (a t) -> p a t", a=1).to_broadcast([P, BU, L])

            def residual(u, par):
                need(dve, "conv_done", u + 1)
                dve.scalar_tensor_tensor(two(seg(h, u)), two(psH[par][:, 0:W]), 1.0 / 3.0, over_batches(posb[:, :]),
                                     ALU.mult, ALU.add).then_inc(s["h0"], 1)

            steps = [0]

            def then(ins):
                steps[0] += 1
                ins.then_inc(s["dve_setup"], 1)
                dve.wait_ge(s["dve_setup"], steps[0])

            dve.memset(eps[:, :], LN_EPS).then_inc(s["eps_ready"], 1)
            dve.wait_ge(s["weights_in"], 48)
            n1 = TAPS // 2 * P
            wc = wconv[:, :, :].rearrange("p j h -> p (j h)")
            then(dve.tensor_tensor(wc[:, 0:n1], wc[:, 0:n1], wconv1[:, :, :].rearrange("p j h -> p (j h)"), ALU.add))
            dve.tensor_tensor(wc[:, 0:n1 // 2], wc[:, 0:n1 // 2], wconv0[:, :, :].rearrange("p j h -> p (j h)"),
                              ALU.add).then_inc(s["conv_w"], 1)
            dve.wait_ge(s["cols_in"], 32)
            c_b0, c_ar, c_ai, c_dv = 0, 3, 4, 5
            t = lambda i: tab[:, i:i + 1]
            tt, ts, stt = dve.tensor_tensor, dve.tensor_scalar, dve.scalar_tensor_tensor
            then(dve.tensor_reduce(t(0), cols[:, 0:3], AX_X, ALU.add))
            then(ts(t(0), t(0), 1.0 / 3.0, None, ALU.mult))
            then(ts(posb[:, :], posb[:, :], t(0), None, ALU.add))

            then(ts(t(0), cols[:, c_ar:c_ar + 1], -1.0, None, ALU.mult))
            then(tt(t(0), t(0), cols[:, c_ar:c_ar + 1], ALU.min))
            then(ts(t(0), t(0), -DAMP_MIN, None, ALU.add))
            then(ts(t(1), t(0), DT / 2, None, ALU.mult))
            then(ts(t(2), cols[:, c_ai:c_ai + 1], DT / 2, None, ALU.mult))
            then(ts(t(3), t(1), -1.0, 1.0, ALU.mult, ALU.add))
            then(tt(t(4), t(2), t(2), ALU.mult))
            then(stt(t(4), t(3), t(3), t(4), ALU.mult, ALU.add))
            then(dve.reciprocal(t(4), t(4)))
            then(tt(t(5), t(3), t(4), ALU.mult))
            then(tt(t(6), t(2), t(4), ALU.mult))
            then(ts(t(3), t(1), 1.0, None, ALU.add))
            then(tt(t(7), t(2), t(6), ALU.mult))
            then(stt(t(8), t(3), t(5), t(7), ALU.mult, ALU.subtract))
            then(tt(t(7), t(2), t(5), ALU.mult))
            then(stt(t(9), t(3), t(6), t(7), ALU.mult, ALU.add))
            then(tt(t(7), t(9), t(9), ALU.mult))
            then(stt(t(10), t(8), t(8), t(7), ALU.mult, ALU.add))
            ts(t(11), t(10), 1e-30, None, ALU.max).then_inc(s["tables"], 1)
            dve.wait_ge(s["tables"], 2)
            then(dve.reciprocal(t(13), t(12)))
            then(stt(t(13), t(11), t(13), t(12), ALU.mult, ALU.add))
            then(ts(t(12), t(13), 0.5, None, ALU.mult))
            then(dve.reciprocal(t(13), t(12)))
            then(ts(t(14), t(10), 0.0, None, ALU.is_equal))
            then(tt(t(15), t(8), t(13), ALU.mult))
            then(tt(t(15), t(15), t(14), ALU.add))
            then(tt(t(16), t(9), t(13), ALU.mult))
            dve.memset(decay[:, :, :], 0.0)
            then(ts(t(5), t(5), DT, None, ALU.mult))
            then(ts(t(6), t(6), DT, None, ALU.mult))
            dve.memset(cosn[:, 0:1], 1.0)
            then(dve.memset(sinn[:, 0:1], 0.0))
            n = 1
            c, sn = 15, 16
            while n < L:
                c2, s2 = (19, 20) if c == 15 else (15, 16)
                ts(tmpn[:, 0:n], sinn[:, 0:n], t(sn), None, ALU.mult)
                ts(tmpn[:, n:2 * n], cosn[:, 0:n], t(sn), None, ALU.mult)
                then(tt(t(17), t(sn), t(sn), ALU.mult))
                stt(cosn[:, n:2 * n], cosn[:, 0:n], t(c), tmpn[:, 0:n], ALU.mult, ALU.subtract)
                stt(sinn[:, n:2 * n], sinn[:, 0:n], t(c), tmpn[:, n:2 * n], ALU.mult, ALU.add)
                stt(t(s2), t(c), 2.0, t(sn), ALU.mult, ALU.mult)
                then(stt(t(c2), t(c), t(c), t(17), ALU.mult, ALU.subtract))
                c, sn = c2, s2
                n *= 2
                if n == 128:
                    residual(0, 0)
            top, low = slice(0, N_STATE), slice(N_STATE, P)
            ts(tmpn[top, 0:L], sinn[top, 0:L], tab[top, 6:7], None, ALU.mult)
            then(ts(tmpn[low, 0:L], sinn[low, 0:L], tab[low, 5:6], None, ALU.mult))
            stt(tin[top, :], cosn[top, 0:L], tab[top, 5:6], tmpn[top, 0:L], ALU.mult, ALU.add)
            stt(tin[low, :], cosn[low, 0:L], tab[low, 6:7], tmpn[low, 0:L], ALU.mult, ALU.subtract)
            dve.tensor_copy(tout[top, :], cosn[top, 0:L])
            ts(tout[low, :], sinn[low, 0:L], -1.0, None, ALU.mult)
            for b in range(BU):
                then(ts(decay[:, b, 1:L], cosn[:, 1:L], 0.0, t(12), ALU.mult, ALU.add))

            dve.wait_ge(s["cst_in"], 16)
            dve.tensor_copy(upper_bf[:, :], const("upper")).then_inc(s["route_bf"], 1)
            dve.memset(ones_bf[:, :], 1.0).then_inc(s["route_bf"], 1)

            def body(u, par):
                v, y = u - 1, u - 2
                if live(y):
                    need(dve, "y1", y + 1)
                    need(dve, "dterm", y + 1)
                    dve.tensor_tensor(seg(h, y), seg(h, y), psY[:, 0:W], ALU.add).then_inc(s["h1"], 1)
                if live(v):
                    need(dve, "rstd1", v + 1)
                    need(dve, "bu", v)
                    need(dve, "dterm", v)
                    dve.tensor_tensor(u1[:, :], psC[:, 0:W], rstd[:, :], ALU.mult).then_inc(s["u1_ready"], 1)
                if live(v):
                    need(dve, "bu", v + 1)
                    need(dve, "scan_done", v)
                    dve.tensor_tensor(two(vin[:, :]), two(psB[:, 0:W]), over_batches(tin[:, :]),
                                      ALU.mult).then_inc(s["vin_ready"], 1)
                if live(y):
                    need(dve, "rstd2_ready", y + 1)
                    dve.tensor_tensor(seg(u2, y), psC2[:, 0:W], rstd2[:, :], ALU.mult).then_inc(s["u2_ready"], 1)
                if live(v):
                    need(dve, "vin_ready", v + 1)
                    need(dve, "state_ready", v)
                    need(dve, "y1", v)
                    dve.tensor_tensor_scan(state[:, :], decay[:, :, :].rearrange("p b t -> p (b t)"), vin[:, :], 0.0,
                                           ALU.mult, ALU.add).then_inc(s["scan_done"], 1)
                if live(u) and not (isinstance(u, int) and u == 0):
                    residual(u, par)
                if live(v):
                    need(dve, "scan_done", v + 1)
                    dve.tensor_tensor(two(state[:, :]), two(state[:, :]), over_batches(tout[:, :]),
                                      ALU.mult).then_inc(s["state_ready"], 1)
                    need(dve, "u1_ready", v + 1)
                    dve.scalar_tensor_tensor(seg(h, v), u1[:, :], cols[:, 5:6], seg(h, v), ALU.mult,
                                             ALU.add).then_inc(s["dterm"], 1)
                if live(y):
                    need(dve, "u2_ready", y + 1)
                    dve.tensor_reduce(msum[:, bass.ds(y * BU, BU)], two(seg(u2, y)), AX_X, ALU.add)\
                       .then_inc(s["msum_ready"], 1)

            units(dve, body, 2)

            g = lambda i: gs[:, i * E:(i + 1) * E]
            g1 = lambda i: gs[:, 7 * E + i:7 * E + i + 1]
            dve.wait_ge(s["wb_in"], WB_IN)
            dve.wait_ge(s["gate_pe"], 1)
            then(stt(g(0), bk[0][0:B, 0:E], 1.0 / L, gate_b[:, :], ALU.mult, ALU.add))
            then(dve.tensor_reduce(g1(0), g(0), AX_X, ALU.max))
            ts(g(1), g(0), g1(0), None, ALU.subtract).then_inc(s["gate_dve"], 1)
            then(ts(g(4), g(0), g1(0), None, ALU.is_equal))
            then(tt(g(4), g(4), const("first_wins")[0:B, 0:E], ALU.mult))
            then(dve.tensor_reduce(g1(1), g(4), AX_X, ALU.max))
            then(ts(g(4), g(4), g1(1), None, ALU.is_equal))
            dve.wait_ge(s["gate_act"], 1)
            then(dve.tensor_reduce(g1(2), g(2), AX_X, ALU.add))
            then(dve.reciprocal(g1(3), g1(2)))
            then(ts(g(3), g(4), g1(3), None, ALU.mult))
            then(tt(g(5), g(4), const("expert_id")[0:B, :], ALU.mult))
            dve.tensor_reduce(pick_f[:, :], g(5), AX_X, ALU.add).then_inc(s["gate_dve"], 1)
            dve.wait_ge(s["gate_pe"], 2)
            dve.tensor_copy(pick[:, :], bk[2][0:1, 0:B]).then_inc(s["pick_ready"], 1)
            dve.tensor_copy(gT[:, :], bk[1][0:E, 0:B]).then_inc(s["gate_dve"], 1)
            dve.wait_ge(s["gate_pe"], 3)
            then(dve.tensor_copy(gate[:, :], bk[3][:, 0:B]))
            dve.tensor_copy(gbias[:, :], bk[4][:, 0:B]).then_inc(s["gate_dve"], 1)
            then(dve.memset(seen[:, :], 0.0))
            then(dve.memset(turn_dve[:, :], 0.0))
            then(dve.tensor_copy(r0["tok"][:, :], const("token")))
            dve.wait_ge(s["gate_dve"], 4)
            dve.wait_ge(s["pads_ready"], PADS)

            def halves(ap, size):
                x = ap.rearrange("p (n two c) -> p n two c", two=2, c=size)
                return x[:, :, 0, :], x[:, :, 1, :]

            def route(ap):
                return ap.rearrange("p (m o) -> p m o", o=1).to_broadcast([P, NT, E])

            def per_expert(ap):
                return ap.rearrange("p (o e) -> p o e", o=1).to_broadcast([P, NT, E])

            def body(u, par):
                w, v_, y, z = u - 1, u - 2, u - 3, u - 4
                wp, vp, yp, zp = 1 - par, par, 1 - par, par
                kf = k[vp][:, :, :].rearrange("p b t -> p (b t)")
                af = a[vp][:, :, :].rearrange("p b t -> p (b t)")

                def level(n, size, b):
                    if not live(v_):
                        return
                    nb = near[:, b * TPB:(b + 1) * TPB, :]
                    need(dve, f"lv{size}", v_ * 2 + b + 1)
                    if size == 1:
                        need(dve, "near_placed", v_ * 4)
                        m = const("diag32").rearrange("p (o c) -> p o c", o=1).to_broadcast([P, TPB, 32])
                        tt(nb, near_at(0, b).rearrange("p (m c) -> p m c", m=TPB), m, ALU.mult)\
                            .then_inc(s["diag_ready"], 1)
                    else:
                        need(dve, "grown", v_ * LV + 2 * (n - 1) + b + 1)
                    block = af if size == 1 else prod[size][:, :]
                    blocks = LP // size
                    tl, tr = halves(block[:, b * blocks:(b + 1) * blocks], 1)
                    ql, qr = halves(qs[vp][:, b * LP:(b + 1) * LP], size)
                    kl, kr = halves(kf[:, b * LP:(b + 1) * LP], size)
                    if size < 64:
                        half = blocks // 2
                        tt(prod[2 * size][:, b * half:(b + 1) * half], tl[:, :, 0], tr[:, :, 0], ALU.mult)
                    else:
                        ql, qr, tl = ql[:, 1:2], qr[:, 1:2], tl[:, 1:2]
                        kl, kr, tr = kl[:, 0:1], kr[:, 0:1], tr[:, 0:1]
                    shape = [P, blocks // 2 if size < 64 else 1, size]
                    tt(qr, qr, tl.to_broadcast(shape), ALU.mult)
                    if size == 1:
                        need(dve, "diag_ready", v_ * 2 + b + 1)
                    last = tt(kl, kl, tr.to_broadcast(shape), ALU.mult)
                    if size < 32:
                        m = const(f"level{size}").bitcast(I32).rearrange("p (o c) -> p o c", o=1)
                        m = m.to_broadcast([P, TPB, 32])
                        src = near_at(n + 1, b).rearrange("p (m c) -> p m c", m=TPB)
                        last = dve.copy_predicated(nb, m, src)
                    last.then_inc(s["grown"], 1)

                def stats(name, n, t, src):
                    for m in range(NT):
                        st = dve.bn_stats(t["stats"][:, m, :], src[:, m, :])
                    st.then_inc(s[f"stats{name}"], 1)

                def aggregate(name, t):
                    for m in range(NT):
                        ag = dve.bn_aggr(t["agg"][:, m, :], t["stats"][:, m, :])
                    ag.then_inc(s[f"agg{name}"], 1)

                def normalise(t, dst, src):
                    for m in range(NT):
                        nm = ts(dst[:, m, :], src[:, m, :], t["agg"][:, m, 0:1], t["rstd"][:, m:m + 1],
                                ALU.subtract, ALU.mult)
                    return nm

                def shift(name, n, t):
                    need(dve, f"rstd{name}", n + 1)
                    need(dve, f"agg{name}", n + 1)
                    stt(t["shift"][:, :], t["agg"][:, :, 0], -1.0, t["rstd"][:, :], ALU.mult, ALU.mult)\
                        .then_inc(s[f"shift{name}"], 1)

                r = r1

                def step(ins):
                    ins.then_inc(s["r_dve"], 1)

                def after(unit, count):
                    need(dve, "r_dve", unit * R_STEPS + count)

                level(0, 1, 0)
                level(0, 1, 1)
                if live(y):
                    need(dve, "av", y + 1)
                    pd = far_ps[:, :, 0:TPB * (P + 1)].rearrange("p b (t f) -> p b t f", t=TPB)
                    ts(den[:, :, :], pd[:, :, :, P], ATTN_EPS, None, ALU.add).then_inc(s["den_ready"], 1)
                level(1, 2, 0)
                if live(y):
                    need(dve, "den_ready", y + 1)
                    dve.reciprocal(rden[:, :, :], den[:, :, :]).then_inc(s["rden_ready"], 1)
                level(1, 2, 1)
                if live(y):
                    need(dve, "rden_ready", y + 1)
                    if live(y, 2):
                        dma_slot(dve, "sent", y, yp)
                    old = by_token(y)
                    for m in range(NT):
                        b, t = m // TPB, m % TPB
                        mx = stt(pay[yp][:, m, P:2 * P], pd[:, b, t, 0:P], rden[:, b, t:t + 1], old[:, m, :],
                                 ALU.mult, ALU.add)
                    mx.then_inc(s["h3"], 1)
                if live(u):
                    need(dve, "ffn_done", u + 1)
                    need(dve, "h2T", u)
                    tt(h2f[:, :], seg(h, u), ffn[:, :], ALU.add).then_inc(s["h2"], 1)
                if live(y):
                    need(dve, "h3", y + 1)
                    stats(4, y, ln[1], pay[yp][:, :, P:2 * P])
                    need(dve, "stats4", y + 1)
                    tt(turn_dve[:, 0:1], turn_dve[:, 1:2], turn_dve[:, 1:2], ALU.add)
                    aggregate(4, ln[1])
                level(2, 4, 0)
                if live(z):
                    need(dve, "ranks", z + 1)
                    need(dve, "ranks_read", z)
                    rk = bk[7][:, 96:96 + (NT + 1) * E].rearrange("p (m e) -> p m e", e=E)
                    step(tt(r["rank"][:, :, :], rk[:, 0:NT, :], per_expert(seen[:, :]), ALU.add))
                level(2, 4, 1)
                if live(y):
                    shift(4, y, ln[1])
                if live(z):
                    after(z, 8)
                    tt(seen[:, :], rk[:, NT, :], seen[:, :], ALU.add).then_inc(s["ranks_read"], 1)
                    tt(r["ranked"][:, :, :], r["rank"][:, :, :], onehot[:, :, :], ALU.mult).then_inc(s["ranked"], 1)
                level(3, 8, 0)
                if live(z):
                    need(dve, "ranked", z + 1)
                    step(dve.tensor_reduce(r0["rank"][:, :], r["ranked"][:, :, :], AX_X, ALU.add))
                    need(dve, "prob_ready", z + 1)
                    dve.tensor_copy(pay[zp][:, :, 2 * P], r0["prob"][:, :])
                    dve.tensor_copy(pay[zp][:, :, 2 * P + 1], r0["tok"][:, :]).then_inc(s["marked"], 1)
                level(3, 8, 1)
                if live(z):
                    after(z, 9)
                    ts(r0["over"][:, :], r0["rank"][:, :], float(CAP), NOWHERE, ALU.is_gt, ALU.mult)
                    tt(r0["slotf"][:, :], r0["rank"][:, :], r0["base"][:, :], ALU.add).then_inc(s["slot_parts"], 1)
                    need(dve, "marked", z + 1)
                    ts(r0["tok"][:, :], r0["tok"][:, :], float(W), None, ALU.add)
                if live(u):
                    need(dve, "h2_ready", u + 1)
                    stats(3, u, ln[0], by_token(u))
                if live(z):
                    need(dve, "slot_parts", z + 1)
                    if live(z, 2):
                        dma_slot(dve, "sent", z, zp)
                    tt(slot[zp][:, :], r0["slotf"][:, :], r0["over"][:, :], ALU.add).then_inc(s["slot_ready"], 1)
                if live(u):
                    need(dve, "stats3", u + 1)
                    tt(turn_dve[:, 0:1], turn_dve[:, 1:2], turn_dve[:, 1:2], ALU.add)
                    aggregate(3, ln[0])
                level(4, 16, 0)
                level(4, 16, 1)
                if live(u):
                    need(dve, "rstd3", u + 1)
                    need(dve, "agg3", u + 1)
                    need(dve, "u3T", u)
                    normalise(ln[0], u3t, by_token(u)).then_inc(s["u3_normed"], 1)
                if live(y):
                    need(dve, "logits", y + 1)
                    step(tt(r["logit"][:, :, :], bk[7][:, 0:NT * E].rearrange("p (m e) -> p m e", m=NT),
                            per_expert(bswitch[:, :]), ALU.add))
                level(5, 32, 0)
                if live(y):
                    after(y, 1)
                    step(dve.tensor_reduce(r0["top"][:, :], r["logit"][:, :, :], AX_X, ALU.max))
                level(5, 32, 1)
                if live(y):
                    after(y, 2)
                    need(dve, "exps_ready", y)
                    tt(r["shifted"][:, :, :], r["logit"][:, :, :], route(r0["top"][:, :]), ALU.subtract)\
                        .then_inc(s["r_shifted"], 1)
                    step(tt(r["first"][:, :, :], r["logit"][:, :, :], route(r0["top"][:, :]), ALU.is_equal))
                level(6, 64, 0)
                if live(y):
                    after(y, 3)
                    step(tt(cand[:, :, 0:E], r["first"][:, :, :],
                            const("first_wins").rearrange("p (m e) -> p m e", e=E), ALU.mult))
                level(6, 64, 1)
                if live(y):
                    after(y, 4)
                    step(dve.tensor_reduce(r0["best"][:, :], cand[:, :, :], AX_X, ALU.max))
                if live(w):
                    need(dve, "q_ready", w + 1)
                    need(dve, "a_ready", w + 1)
                    if live(y):
                        need(dve, "lv128", y + 1)
                    tt(qs[wp][:, :], q[wp][:, :, :].rearrange("p b t -> p (b t)"),
                       a[wp][:, :, :].rearrange("p b t -> p (b t)"), ALU.mult).then_inc(s["qs_ready"], 1)
                if live(y):
                    after(y, 5)
                    need(dve, "ranks", y)
                    tt(onehot[:, :, :], cand[:, :, 0:E], route(r0["best"][:, :]), ALU.is_equal)\
                        .then_inc(s["onehot_ready"], 1)
                    step(stt(r0["base"][:, :], r0["best"][:, :], -float(CAP), const("slot_of"), ALU.mult, ALU.add))
                if live(w):
                    need(dve, "v_mm", w + 1)
                    tt(v[wp][:, :, 0:P], bk[1][:, :].rearrange("p (m f) -> p m f", m=NT),
                       bv[:, :].rearrange("p (o f) -> p o f", o=1).to_broadcast([P, NT, P]), ALU.add)\
                        .then_inc(s["v_ready"], 1)
                if live(y):
                    need(dve, "exps_ready", y + 1)
                    step(dve.tensor_reduce(r0["total"][:, :], r["exps"][:, :, :], AX_X, ALU.add))
                    after(y, 7)
                    need(dve, "pay_u", y * NT)
                    dve.reciprocal(r0["prob"][:, :], r0["total"][:, :]).then_inc(s["prob_ready"], 1)

            units(dve, body, 4)

            def bias(e):
                return bexp[:, bass.ds(e, 1), :].rearrange("p e f -> p (e f)")

            def finish(t, par):
                e = 2 * t + par
                need(dve, "expert_y", e + 1)
                if not isinstance(t, int) or t > 0:
                    dve.wait_ge(s[f"done{par}"], t * (16 * EM))
                for m in range(EM):
                    f = stt(res[par][:, m, :], bias(e), rows[par][:, m, 2 * P:2 * P + 1],
                            bk[2][:, m * P:(m + 1) * P], ALU.mult, ALU.add)
                f.then_inc(s["res_mm"], 1)
                dve.tensor_copy(where[par][:, :], rows[par][:, :, 2 * P + 1]).then_inc(s["where_ready"], 1)
                need(dve, "res_mm", e + 1)
                tt(res[par][:, :, :], res[par][:, :, :], rows[par][:, :, P:2 * P], ALU.add).then_inc(s["res_ready"], 1)

            def finish_rest(t):
                need(dve, "rest_y", t + 1)
                if not isinstance(t, int) or t > 0:
                    dve.wait_ge(s["rest_done"], t * 16)
                for half in range(2):
                    own = slice(half * HALF, half * HALF + REST)
                    f = stt(rest_res[own, :], bias(2 * t + half)[own], rest[own, 2 * P:2 * P + 1], bk[3][own, 0:P],
                            ALU.mult, ALU.add)
                f.then_inc(s["rest_mm"], 1)
                dve.tensor_copy(rest_where[:, :], rest[:, 2 * P + 1:2 * P + 2]).then_inc(s["rest_where_ready"], 1)
                need(dve, "rest_mm", t + 1)
                for half in range(2):
                    own = slice(half * HALF, half * HALF + REST)
                    f = tt(rest_res[own, :], rest_res[own, :], rest[own, P:2 * P], ALU.add)
                f.then_inc(s["rest_ready"], 1)

            finish(0, 0)
            finish(0, 1)
            finish_rest(0)
            with dve.Fori(1, E // 2) as t:
                finish(t, 0)
                finish(t, 1)
                finish_rest(t)


def kernel(**inputs):
    import numpy as np
    import concourse.bacc as _bacc
    from concourse import mybir as _mybir
    from concourse.bass_utils import run_bass_kernel_spmd as _run

    i = {k: np.asarray(v) for k, v in inputs.items()}

    def conv_w(w):
        return np.ascontiguousarray(w.T.reshape(-1, P, P).transpose(1, 0, 2))

    col = lambda a: a.reshape(-1, 1)
    x = i["x"]
    x2 = np.ascontiguousarray(np.concatenate([x[:, 0:XT], x[:, 1:S_IN]], axis=2).transpose(2, 0, 1))
    z = np.zeros((P, 1), np.float32)
    cols = [col(i["L0_tok_b0"]), col(i["L0_tok_b1"]), col(i["L0_tok_b2"]),
            col(np.concatenate([i["L0_attn_A_real"]] * 2)), col(np.concatenate([i["L0_attn_A_imag"]] * 2)),
            col(i["L0_attn_D_vec"]), col(i["L1_attn_bq"]), col(i["L1_attn_bk"]), col(i["L1_attn_ba"])]
    cols = np.concatenate(cols + [z] * (16 - len(cols)), axis=1)
    arrays = {
        "x2": x2, "wconv2": conv_w(i["L0_tok_W2"]), "wconv1": conv_w(i["L0_tok_W1"]), "wconv0": conv_w(i["L0_tok_W0"]),
        "cols": cols, "pos": np.ascontiguousarray(i["L0_tok_pos"][0, 0:L].T),
        "cst": constants(),
        "wg": i["L0_ffn_Wg"], "bg": np.tile(i["L0_ffn_bg"], (B, 1)), "be": i["L0_ffn_be"], "we": i["L0_ffn_We"],
        "bv": np.tile(i["L1_attn_bv"], (P, 1)),
        "wqkav": np.ascontiguousarray(np.stack([i[f"L1_attn_W{n}"].T for n in "qkav"], axis=1)),
        "wswitch": np.ascontiguousarray(i["L1_ffn_switch_w"].T), "bswitch": np.tile(i["L1_ffn_switch_b"], (P, 1)),
        "wexp": np.ascontiguousarray(i["L1_ffn_expert_w"].transpose(2, 0, 1)),
        "bexp": np.tile(i["L1_ffn_expert_b"][None], (P, 1, 1)),
        "ssm_in": np.ascontiguousarray(np.concatenate([i["L0_attn_B_mat"]] * 2).T),
        "ssm_out": np.ascontiguousarray(np.concatenate([i["L0_attn_C_mat"].T] * 2)),
    }
    nc = _bacc.Bacc("TRN2", target_bir_lowering=False, num_devices=1)
    args, sent = {}, {}
    for name, a in arrays.items():
        sent[f"in_{name}"] = a
        args[name] = nc.dram_tensor(f"in_{name}", a.shape, _mybir.dt.from_np(a.dtype), kind="ExternalInput").ap()
    slots = nc.dram_tensor("slots", (E * CAP, ROW), F32, kind="Internal").ap()
    out = nc.dram_tensor("out_0", (NTOK, P), F32, kind="ExternalOutput").ap()
    bass_audio_tower_kernel(nc, args, slots, out)
    r = _run(nc, [sent], core_ids=[0])
    return r.results[0]["out_0"].reshape(B, L, P)


def constants():
    import numpy as np
    p = np.arange(P)
    t = np.arange(32)[None, :]
    j = (p % 32)[:, None]
    eye = np.eye(P)
    tile = np.arange(NT)[None, :]
    valid = np.where(tile % TPB == 1, L - TILE, TILE)
    parts = {
        "ident": eye, "center": eye - 1.0 / P, "mean": np.full((P, P), 1.0 / P), "ones": np.ones((P, P)),
        "upper": (p[:, None] <= p[None, :]), "diag32": j == t,
        "first_wins": ((p[:, None] < valid)[:, :, None] * (E - np.arange(E))).reshape(P, NT * E),
        "expert_id": np.tile(np.arange(E), (P, 1)),
        "token": p[:, None] + tile // TPB * L + tile % TPB * TILE,
        "slot_of": E * CAP - 1 + NOWHERE * (p[:, None] >= valid),
    }
    for s in LEVELS:
        parts[f"level{s}"] = (j // (2 * s) == t // (2 * s)) & (j % (2 * s) < s) & (t % (2 * s) >= s)
    return np.concatenate([np.asarray(parts[n], np.float32) for n, _ in CONSTS], axis=1)
```
